# Optimizing a Trainium2 kernel written in Bass

```python
import numpy as np
import jax
import jax.numpy as jnp

def _softmax(x, axis=-1):
    return jax.nn.softmax(x, axis=axis)

def _gelu(x):
    return jax.nn.gelu(x, approximate=True)

def _silu(x):
    return jax.nn.silu(x)

def _sigmoid(x):
    return jax.nn.sigmoid(x)

def _layernorm(x, axis=-1, eps=1e-05):
    m = jnp.mean(x, axis=axis, keepdims=True)
    v = jnp.var(x, axis=axis, keepdims=True)
    return (x - m) / jnp.sqrt(v + eps)

def _scatter_add(tgt, idx, src, axis=0):
    return tgt.at[idx].add(src)

def _segment_sum(src, seg, n):
    return jax.ops.segment_sum(src, seg, n)
kernel_name = 'mk_gnn_resnorm_d4_gnn_r16_69f51c'

def setup_inputs(seed: int=0):
    np.random.seed(seed)
    _w = jnp.asarray

    def _rec_inputs():
        import jax
        import jax.numpy as jnp
        _gk = jax.random.key(seed)
        x = -0.0003713 + 1 * jax.random.normal(jax.random.fold_in(_gk, 1), (6250, 128), jnp.float32)
        _s = jax.random.randint(jax.random.fold_in(_gk, 2), (100000,), 0, 6250, jnp.int32)
        _d = jax.random.randint(jax.random.fold_in(_gk, 3), (100000,), 0, 6250, jnp.int32)
        _loop = jnp.arange(6250, dtype=jnp.int32)
        src = jnp.concatenate([_s, _d, _loop])
        dst = jnp.concatenate([_d, _s, _loop])
        _o = jnp.argsort(dst, stable=True)
        src = src[_o]
        dst = dst[_o]
        edge_attr_16 = 0.000254156 + 0.999948 * jax.random.normal(jax.random.fold_in(_gk, 11), (206250, 16), jnp.float32)
        return (x, src, dst, edge_attr_16)
    x, src, dst, edge_attr_16 = _rec_inputs()

    def _L0_gnn_setup():
        import jax, jax.numpy as jnp
        import numpy as np
        N_NODES = 6250
        N_EDGES = 50000
        D_IN = 128
        D_OUT = 128
        E_DIM = 16
        key = jax.random.key(seed)
        k1, k2, k3, k4, k5 = jax.random.split(key, 5)
        x = jax.random.normal(k1, (N_NODES, D_IN), dtype=jnp.float32)
        edge_index = jax.random.randint(k2, (2, N_EDGES), 0, N_NODES, dtype=jnp.int64)
        edge_attr = jax.random.normal(k3, (N_EDGES, E_DIM), dtype=jnp.float32)
        W = jax.random.uniform(k4, (D_IN, D_OUT), dtype=jnp.float32, minval=-1.0, maxval=1.0) * float(np.sqrt(6.0 / (D_IN + D_OUT)))
        edge_w = jax.random.uniform(k5, (E_DIM, D_OUT), dtype=jnp.float32, minval=-1.0, maxval=1.0) * float(np.sqrt(6.0 / (E_DIM + D_OUT)))
        b = jnp.zeros((D_OUT,), dtype=jnp.float32)
        return {'x': x, 'edge_index': edge_index, 'edge_attr': edge_attr, 'W': W, 'edge_w': edge_w, 'b': b}
    _L0_gnn_all = _L0_gnn_setup()
    _L0_gnn_in = {k: v for k, v in _L0_gnn_all.items() if k in ('W', 'edge_w', 'b')}
    del _L0_gnn_all

    def _L1_gnn_setup():
        import jax, jax.numpy as jnp
        import numpy as np
        N_NODES = 3125
        N_EDGES = 37500
        D = 128
        H = 128
        key = jax.random.key(seed)
        k1, k2, k3, k4 = jax.random.split(key, 4)
        x = jax.random.normal(k1, (N_NODES, D), dtype=jnp.float32)
        edge_index = jax.random.randint(k2, (2, N_EDGES), 0, N_NODES, dtype=jnp.int64)
        scale = 1.0 / np.sqrt(D)
        W_l = jax.random.normal(k3, (H, D), dtype=jnp.float32) * scale
        b_l = jnp.zeros((H,), dtype=jnp.float32)
        W_r = jax.random.normal(k4, (H, D), dtype=jnp.float32) * scale
        return {'x': x, 'edge_index': edge_index, 'W_l': W_l, 'b_l': b_l, 'W_r': W_r}
    _L1_gnn_all = _L1_gnn_setup()
    _L1_gnn_in = {k: v for k, v in _L1_gnn_all.items() if k in ('W_l', 'b_l', 'W_r')}
    del _L1_gnn_all

    def _L2_gnn_setup():
        import jax, jax.numpy as jnp
        import numpy as np
        EPS = 1e-06
        key = jax.random.key(seed)
        k1, k2, k3 = jax.random.split(key, 3)
        N, E, CIN, COUT = (3125, 50000, 128, 128)
        x = jax.random.normal(k1, (N, CIN), dtype=jnp.float32)
        edge_index = jax.random.randint(k2, (2, E), 0, N, dtype=jnp.int64)
        limit = float(np.sqrt(6.0 / (CIN + COUT)))
        weight = jax.random.uniform(k3, (CIN, COUT), minval=-limit, maxval=limit, dtype=jnp.float32)
        bias = jnp.zeros((COUT,), dtype=jnp.float32)
        return {'x': x, 'edge_index': edge_index, 'weight': weight, 'bias': bias}
    _L2_gnn_all = _L2_gnn_setup()
    _L2_gnn_in = {k: v for k, v in _L2_gnn_all.items() if k in ('weight', 'bias')}
    del _L2_gnn_all

    def _L3_gnn_setup():
        import jax, jax.numpy as jnp
        import numpy as np
        N_NODES = 6250
        N_EDGES = 100000
        D_IN = 128
        D_HID = 128
        BN_EPS = 1e-05
        key = jax.random.key(seed)
        ks = jax.random.split(key, 8)
        x = jax.random.normal(ks[0], (N_NODES, D_IN), dtype=jnp.float32)
        edge_index = jax.random.randint(ks[1], (2, N_EDGES), 0, N_NODES, dtype=jnp.int64)
        sw = 1.0 / np.sqrt(D_IN)
        gcn_w = jax.random.normal(ks[2], (D_IN, D_HID), dtype=jnp.float32) * sw
        lin_w = jax.random.normal(ks[3], (D_IN, D_HID), dtype=jnp.float32) * sw
        gate_w = jax.random.normal(ks[4], (D_HID, D_HID), dtype=jnp.float32) * sw
        return {'x': x, 'edge_index': edge_index, 'gcn_w': gcn_w, 'gcn_b': jnp.zeros((D_HID,), jnp.float32), 'lin_w': lin_w, 'lin_b': jnp.zeros((D_HID,), jnp.float32), 'gate_w': gate_w, 'gate_b': jnp.zeros((D_HID,), jnp.float32), 'bn_gamma': jnp.ones((D_HID,), jnp.float32), 'bn_beta': jnp.zeros((D_HID,), jnp.float32)}
    _L3_gnn_all = _L3_gnn_setup()
    _L3_gnn_in = {k: v for k, v in _L3_gnn_all.items() if k in ('gcn_w', 'gcn_b', 'lin_w', 'lin_b', 'gate_w', 'gate_b', 'bn_gamma', 'bn_beta')}
    del _L3_gnn_all
    return {'x': x, 'src': src, 'dst': dst, 'edge_attr_16': edge_attr_16, 'L0_gnn_W': _L0_gnn_in['W'], 'L0_gnn_edge_w': _L0_gnn_in['edge_w'], 'L0_gnn_b': _L0_gnn_in['b'], 'L1_gnn_W_l': _L1_gnn_in['W_l'], 'L1_gnn_b_l': _L1_gnn_in['b_l'], 'L1_gnn_W_r': _L1_gnn_in['W_r'], 'L2_gnn_weight': _L2_gnn_in['weight'], 'L2_gnn_bias': _L2_gnn_in['bias'], 'L3_gnn_gcn_w': _L3_gnn_in['gcn_w'], 'L3_gnn_gcn_b': _L3_gnn_in['gcn_b'], 'L3_gnn_lin_w': _L3_gnn_in['lin_w'], 'L3_gnn_lin_b': _L3_gnn_in['lin_b'], 'L3_gnn_gate_w': _L3_gnn_in['gate_w'], 'L3_gnn_gate_b': _L3_gnn_in['gate_b'], 'L3_gnn_bn_gamma': _L3_gnn_in['bn_gamma'], 'L3_gnn_bn_beta': _L3_gnn_in['bn_beta']}

def reference(x, src, dst, edge_attr_16, L0_gnn_W, L0_gnn_edge_w, L0_gnn_b, L1_gnn_W_l, L1_gnn_b_l, L1_gnn_W_r, L2_gnn_weight, L2_gnn_bias, L3_gnn_gcn_w, L3_gnn_gcn_b, L3_gnn_lin_w, L3_gnn_lin_b, L3_gnn_gate_w, L3_gnn_gate_b, L3_gnn_bn_gamma, L3_gnn_bn_beta):
    import jax
    import jax.numpy as jnp

    def _L0_gnn_ref(x, edge_index, edge_attr, W, edge_w, b):
        import jax, jax.numpy as jnp
        import numpy as np
        N_NODES = 6250
        N_EDGES = 50000
        D_IN = 128
        D_OUT = 128
        E_DIM = 16
        src, dst = (edge_index[0], edge_index[1])
        xw = x @ W
        ew = edge_attr @ edge_w
        msg = xw[src] * ew
        out = jax.ops.segment_sum(msg, dst, num_segments=x.shape[0])
        out = out + b
        return out

    def _L1_gnn_ref(x, edge_index, W_l, b_l, W_r):
        import jax, jax.numpy as jnp
        import numpy as np
        N_NODES = 3125
        N_EDGES = 37500
        D = 128
        H = 128
        src = edge_index[0]
        dst = edge_index[1]
        n = x.shape[0]
        msgs = x[src]
        agg_sum = jax.ops.segment_sum(msgs, dst, num_segments=n)
        deg = jax.ops.segment_sum(jnp.ones((src.shape[0],), dtype=x.dtype), dst, num_segments=n)
        agg = agg_sum / jnp.maximum(deg, 1.0)[:, None]
        out = agg @ W_l.T + b_l + x @ W_r.T
        return out

    def _L2_gnn_ref(x, edge_index, weight, bias):
        import jax, jax.numpy as jnp
        import numpy as np
        EPS = 1e-06
        N = x.shape[0]
        src, dst = (edge_index[0], edge_index[1])
        ones = jnp.ones(src.shape, dtype=x.dtype)
        src_deg = jax.ops.segment_sum(ones, src, num_segments=N)
        dst_deg = jax.ops.segment_sum(ones, dst, num_segments=N)
        src_inv = jax.lax.rsqrt(src_deg + EPS)
        dst_inv = jax.lax.rsqrt(dst_deg + EPS)
        edge_norm = src_inv[src] * dst_inv[dst]
        msg = x[src] * edge_norm[:, None]
        aggregated = jax.ops.segment_sum(msg, dst, num_segments=N)
        return aggregated @ weight + bias

    def _L3_gnn_ref(x, edge_index, gcn_w, gcn_b, lin_w, lin_b, gate_w, gate_b, bn_gamma, bn_beta):
        import jax, jax.numpy as jnp
        import numpy as np
        N_NODES = 6250
        N_EDGES = 100000
        D_IN = 128
        D_HID = 128
        BN_EPS = 1e-05
        N = x.shape[0]
        loop = jnp.arange(N, dtype=edge_index.dtype)
        src = jnp.concatenate([edge_index[0], loop])
        dst = jnp.concatenate([edge_index[1], loop])
        deg = jax.ops.segment_sum(jnp.ones(src.shape, x.dtype), dst, num_segments=N)
        dinv = jax.lax.rsqrt(jnp.maximum(deg, 1e-12))
        norm = dinv[src] * dinv[dst]
        h = x @ gcn_w
        msg = h[src] * norm[:, None]
        z = jax.ops.segment_sum(msg, dst, num_segments=N) + gcn_b
        z = jnp.tanh(z)
        g = jax.nn.sigmoid(z @ gate_w + gate_b)
        xl = x @ lin_w + lin_b
        out = jax.nn.relu((1.0 - g) * xl + g * z)
        mean = out.mean(axis=0)
        var = out.var(axis=0)
        out = (out - mean) * jax.lax.rsqrt(var + BN_EPS) * bn_gamma + bn_beta
        return out
    edge_index = jnp.stack([src, dst])
    x = _layernorm(x + _L0_gnn_ref(x, edge_index, edge_attr_16, L0_gnn_W, L0_gnn_edge_w, L0_gnn_b), axis=-1)
    x = _layernorm(x + _L1_gnn_ref(x, edge_index, L1_gnn_W_l, L1_gnn_b_l, L1_gnn_W_r), axis=-1)
    x = _layernorm(x + _L2_gnn_ref(x, edge_index, L2_gnn_weight, L2_gnn_bias), axis=-1)
    x = _layernorm(x + _L3_gnn_ref(x, edge_index, L3_gnn_gcn_w, L3_gnn_gcn_b, L3_gnn_lin_w, L3_gnn_lin_b, L3_gnn_gate_w, L3_gnn_gate_b, L3_gnn_bn_gamma, L3_gnn_bn_beta), axis=-1)
    return x

_drawn_inputs = setup_inputs


def setup_inputs(seed=0):
    import zlib

    import numpy as np

    out = dict(_drawn_inputs(seed))
    spreads = {'L0_gnn_b': (0.0, 0.1),
     'L1_gnn_b_l': (0.0, 0.1),
     'L2_gnn_bias': (0.0, 0.1),
     'L3_gnn_gcn_b': (0.0, 0.1),
     'L3_gnn_lin_b': (0.0, 0.1),
     'L3_gnn_gate_b': (0.0, 0.636),
     'L3_gnn_bn_gamma': (1.0, 0.2),
     'L3_gnn_bn_beta': (0.0, 0.1)}
    factors = {}
    for name, (base, spread) in spreads.items():
        noise = np.random.default_rng([zlib.crc32(name.encode()), seed]).standard_normal(out[name].shape)
        drawn = base * np.exp(spread * noise) if base else spread * noise
        out[name] = jnp.asarray(drawn.astype(out[name].dtype))
    for name, factor in factors.items():
        out[name] = (out[name] * factor).astype(out[name].dtype)
    return out
```

```python
from contextlib import ExitStack

import concourse.bass as bass
from concourse import mybir

F32 = mybir.dt.float32
F16 = mybir.dt.float16
I32 = mybir.dt.int32
ALU = mybir.AluOpType
ACT = mybir.ActivationFunctionType
AX = mybir.AxisListType

N = 6250
E = 206250
D = 128
ED = 16
P = 128
NB = -(-N // P)
NP = NB * P
T8 = 8
NH = 2 * -(-E // (2 * T8 * P))
NI = NH // 2
T = NH * T8
GN = 8
GH = 4
GT = 4
SN = GN * GH
G = NH * GH
GC = -(-(G + 1) // P)
W = GN * NB
TT = T + GT
WIN = 128
YW = NP + WIN
BT = 7
NT = NB // BT
CH = 16
CN = CH * SN
NPAIR = NP // (2 * CN)
TAIL = NP - 2 * NPAIR * CN
SCALE = 1024.0
LAST = N - (NB - 1) * P
NCH = 2 * NPAIR + 1
CB = CN // P
(W_L0, W_L1, W_R1, W_L2, W_GCN, W_LIN, W_GATE) = range(7)
(B_L0, B_L1, B_L2, B_GCN, B_LIN, B_GATE, BN_GAMMA, BN_BETA) = range(8)


def build(nc, xT_d, x_d, ea_d, idx_d, src_d, dst_d, first_d, half_d, w_d, vec_d, out_d):
    DVE_ONLY = [mybir.EngineType.DVE]
    ctx = ExitStack()
    with ctx:
        def sb(name, shape, dt=F32):
            return ctx.enter_context(nc.sbuf_tensor(name, shape, dt))

        def sem(name):
            return ctx.enter_context(nc.semaphore(name))

        xw_d = nc.dram_tensor("xw", [NP, D], F32, kind="Internal").ap()
        at_d = nc.dram_tensor("at", [NH, P, NB * SN], F16, kind="Internal").ap()
        x3_d = nc.dram_tensor("x3", [NP, D], F32, kind="Internal").ap()
        start_d = nc.dram_tensor("group_start", [GC, P], I32, kind="Internal").ap()

        x = sb("x", [P, NB, D])
        y = sb("y", [P, NB, D])
        ident = sb("ident", [P, P])
        ones = sb("ones", [P, P])
        ones16 = sb("ones16", [P, P], F16)
        wts = sb("wts", [P, 7, D])
        vecs = sb("vecs", [P, 8, D])
        BIG = sb("big", [P, 2 * CH * NB * SN], F16)
        big_at = [0]

        def part(shape, dt):
            n = 1
            for s in shape[1:]:
                n *= s
            size = n * (2 if dt == F32 or dt == I32 else 1)
            a = BIG[0:shape[0], big_at[0]:big_at[0] + size]
            big_at[0] += size
            if dt != F16:
                a = a.bitcast(dt)
            if len(shape) == 3:
                a = a.rearrange("p (a b) -> p a b", b=shape[2])
            return a

        gath = part([P, 2 * T8, D], F32)
        msg = part([P, 2 * T8, D], F32)
        hot_win = part([P, 2 * T8, WIN], F32)
        dist = part([P, 2 * T8, WIN], F32)
        edge_w = part([P, T8, D], F32)
        ea = part([P, 2, P], F32)
        key = part([P, TT], F32)
        src_lo = part([P, TT], F32)
        rel = part([P, T + T8], F32)
        half_i = part([P, NH], I32)
        src_i = part([P, T], I32)
        src_hi_i = msg.rearrange("p t f -> p (t f)")[:, 0:T].bitcast(I32)
        dst_i = part([P, T], I32)
        first_i = part([P, T], I32)
        first_f = part([P, T], F32)
        win_tab = part([1, NH], I32)
        group_key = part([P, G], F32)
        hot_lo = part([P, 2 * GH * GT, P], F16)
        start_tab = part([1, GC * P], I32)
        assert big_at[0] <= 2 * CH * NB * SN, big_at[0]
        at = [BIG[:, 0:CH * NB * SN], BIG[:, CH * NB * SN:]]

        yT = sb("yT", [P, YW])
        parts = yT[:, 0:NP].bitcast(F16).rearrange("p (s b f) -> p s b f", s=2, f=D)
        hot_key = y[:, :, :].rearrange("p b f -> p (b f)").bitcast(F16)[:, 0:2 * GH * GT * W].rearrange("p (s f) -> p s f", f=W)
        tmp = sb("tmp", [P, 5, BT * D])
        stage = tmp[:, 0:4, :].rearrange("p a b -> p (a b)")[:, 0:NB * SN].bitcast(F16).rearrange("p (h n) -> p h n", h=2)
        flat = tmp[:, :, :].rearrange("p a b -> p (a b)")
        xn = [tmp[:, k, :].rearrange("p (b f) -> p b f", f=D) for k in (0, 1)]
        xs = [tmp[:, k, :].rearrange("p (b f) -> p b f", f=D) for k in (2, 3)]
        xnT = tmp[:, 4, :].rearrange("p (b f) -> p b f", f=D)
        aggT, zpre, zT, gate = ([flat[:, (2 * k + c) * CN:(2 * k + c + 1) * CN] for c in range(2)] for k in range(4))
        deg_row = flat[0:1, 4 * CN:6 * CN].rearrange("p (c n) -> p c n", c=2)
        bn_row = flat[:, 0:4 * D].rearrange("p (k f) -> p k f", f=D)
        less = tmp[:, :, :].rearrange("p a b -> p (a b)")[:, 0:T]
        sdeg_part = sb("sdeg_part", [P, NCH, NB])
        small = sb("small", [P, 11, NB])
        deg, sdeg, scale_l1, src_l2, dst_l2, src_l3, dst_l3, self_l3 = (small[:, k, :] for k in range(8))
        roots = small[:, 8:11, :]
        stats = sb("stats", [P, 2, BT, 6])
        mv_turn = sb("mv_turn", [P, 2, BT, 2])
        mean_var = sb("mean_var", [P, NB, 2])
        rstd = sb("rstd", [P, NB])
        shift = sb("shift", [P, NB])
        eps_ln = sb("eps_ln", [P, 4])
        valid = sb("valid", [P, 1])
        idx = sb("idx", [P, 2, T8], I32)
        start_i = sb("start_i", [P, GC], I32)
        start_f = sb("start_f", [P, GC])
        group_dst = sb("group_dst", [P, GC])
        rel_key = sb("rel_key", [P, 2 * GH, GT])
        cols_key = sb("cols_key", [P, W], F16)
        cols_p = sb("cols_p", [P, P], F16)
        cols_pf = sb("cols_pf", [P, P])

        PB = ctx.enter_context(nc.psum_tensor("pb", [P, 8, 512], F32))

        s_in = {n: sem("in_" + n) for n in ("w", "edge_w", "xT", "src", "dst", "first", "first_b", "half_b", "x", "start")}
        s_const = sem("consts_made")
        s_rowgo, s_rowxw, s_rowev, s_rowst = (sem("xw_" + n) for n in ("stage", "mm", "evac", "stored"))
        s_zero = sem("yT_zeroed")
        s_tab = sem("dve_table_step")
        s_start_st = sem("group_start_stored")
        s_idx = [sem(f"idx_in{h}") for h in range(2)]
        s_gath = [sem(f"gathered{h}") for h in range(2)]
        s_seen = sem("gather_go")
        s_ea = [sem(f"ea_in{h}") for h in range(2)]
        s_ew = [sem(f"ew_done{q}") for q in range(2)]
        s_msg = [sem(f"msg_done{h}") for h in range(2)]
        s_hotw = sem("hot_win_done")
        s_dist = sem("dist_done")
        s_win = [sem(f"win_mm{h}") for h in range(2)]
        s_add = [sem(f"yT_added{h}") for h in range(2)]
        s_rel = [sem(f"rel_key{h}") for h in range(2)]
        s_hot = [sem(f"hot_ready{h}") for h in range(2)]
        s_amm = [sem(f"a_mm{h}") for h in range(2)]
        s_aev = [sem(f"a_evac{j}") for j in range(GH)]
        s_ast = [sem(f"a_stored{h}") for h in range(2)]
        s_fin = {n: sem("l0_" + n) for n in ("bias", "stage", "mm", "add", "stats")}
        def sems(prefix, names):
            return {n: sem(prefix + n) for n in names.split()}

        s_norm = sems("norm_", "sqrt recip ready")
        s_walk = {1: sems("walk1_", "xn0 xn1 xs0 xs1 hi0 hi1 lo tp0 tp1 xnT lin yb0 yb1 y"),
                  2: sems("walk2_", "xn0 xn1 xs0 xs1 hi0 hi1 lo yb0 yb1"),
                  3: sems("walk3_", "xn0 xn1 xs0 xs1 hi0 hi1 lo tp0 tp1 xnT lin y st0 st1"),
                  4: sems("walk4_", "xn0 xn1 st0 st1")}
        S = sems("dense_", "at0 at1 main0 main1 evac0 evac1 lin0 lin1 y0 y1 stats0 stats1")
        s_deg = sems("deg_", "mm0 mm1 row0 row1 col0 col1 red0 red1")
        s_gated = sems("gated_", "z0 z1 zt0 zt1 zts0 zts1 gate0 gate1 g0 g1 mix0 mix1")
        s_root = sem("roots")
        s_past = sem("dve_past_wait")
        s_bn = sem("bn_dve")
        s_bn_pe = sem("bn_pe")
        s_bn_act = sem("bn_act")
        s_bn_pool = sem("bn_pool")
        s_x3 = sem("x3_back")

        block = ctx.enter_context(nc.Block())
        parts_v = [parts[:, k] for k in range(2)]
        at_v = [a.rearrange("p (c h d) -> p c h d", h=NB, d=SN) for a in at]
        BN_SRC = {1: x, 2: y, 3: y, 4: y}
        SRC_SCALE = {2: src_l2, 3: src_l3}
        WGT = {1: W_L1, 2: W_L2, 3: W_GCN}
        DST_SCALE = {1: scale_l1, 2: dst_l2, 3: dst_l3}

        def walk(eng, fn):
            with eng.Fori(0, NT // 2) as p:
                for s in range(2):
                    fn(2 * p + s, s, p)
            if NT % 2:
                fn(NT - 1, 0, NT // 2)

        def of(k, c, p):
            return (k - 1) * (NPAIR + 1 - c) + p

        def blocks(a, t):
            return a[:, bass.ds(t * BT, BT), :]

        def chunks(eng, fn, tail):
            with eng.Fori(0, NPAIR) as p:
                fn(p, (0, 1), CB)
            fn(NPAIR, (0,), TAIL // P)

        big32 = BIG[:, :].bitcast(F32)
        sq = big32[:, 0:NP].rearrange("p (b f) -> p b f", f=D)
        x3b = big32[:, NP:2 * NP].rearrange("p (b f) -> p b f", f=D)
        xwS = gath

        @block.sync
        def _(sp):
            sp.dma_start(wts[:, :, :], w_d[0:7].rearrange("w k n -> k w n")).then_inc(s_in["w"], 16)
            sp.wait_ge(s_const, 1)
            for t in range(T8):
                sp.dma_start(edge_w[ED * t:ED * t + ED, t, :], w_d[7, 0:ED, :]).then_inc(s_in["edge_w"], 16)
            sp.dma_start(yT[:, 0:NP], xT_d).then_inc(s_in["xT"], 16)
            sp.dma_start(src_i, src_d).then_inc(s_in["src"], 16)
            sp.dma_start(dst_i, dst_d).then_inc(s_in["dst"], 16)
            sp.dma_start(first_i, first_d.broadcast_to([P, T])).then_inc(s_in["first_b"], 16)
            sp.dma_start(half_i, half_d.broadcast_to([P, NH])).then_inc(s_in["half_b"], 16)
            sp.dma_start(win_tab[:, :], half_d).then_inc(s_in["first"], 16)
            sp.dma_start(vecs[:, :, :], vec_d.broadcast_to([P, 8, D])).then_inc(s_in["w"], 16)
            sp.dma_start(x[:, 0:NB - 1, :], x_d[0:(NB - 1) * P, :].rearrange("(b p) f -> p b f", p=P)).then_inc(s_in["x"], 16)
            sp.wait_ge(s_const, 2)
            sp.dma_start(x[0:LAST, NB - 1, :], x_d[(NB - 1) * P:N, :]).then_inc(s_in["x"], 16)
            with sp.Fori(0, NT) as i:
                sp.wait_ge(s_rowev, 2 * i + 2)
                sp.dma_start(xw_d[bass.ds(i * (BT * P), BT * P), :].rearrange("(b p) f -> p b f", p=P),
                             xwS[:, T8:T8 + BT, :]).then_inc(s_rowst, 16)
            sp.wait_ge(s_tab, 8)
            with nc.allow_non_contiguous_dma(reason="896 counts, once"):
                sp.dma_start(start_d.rearrange("c p -> p c"), start_i[:, :]).then_inc(s_start_st, 16)
            sp.wait_ge(s_start_st, 16)
            sp.dma_start(start_tab[:, :].rearrange("o (c p) -> o c p", p=P), start_d.rearrange("(o c) p -> o c p", o=1)).then_inc(s_in["start"], 16)
            sp.dma_start(ea[:, 0, :], ea_d[0]).then_inc(s_ea[0], 16)
            with sp.Fori(0, NI) as i:
                for h in range(2):
                    sp.wait_ge(s_gath[h], i * (16 * T8))
                    sp.dma_start(idx[:, h, :], idx_d[bass.ds(2 * i + h, 1), :, :].rearrange("o p t -> (o p) t")).then_inc(s_idx[h], 16)
                    if h == 0:
                        sp.wait_ge(s_ew[1], 2 * i)
                        sp.dma_start(ea[:, 1, :], ea_d[bass.ds(2 * i + 1, 1), :, :].rearrange("o k e -> (o k) e")).then_inc(s_ea[1], 16)
                    else:
                        sp.wait_ge(s_ew[1], 2 * i + 1)
                        sp.dma_start(ea[:, 0, :], ea_d[bass.ds(2 * i + 2, 1), :, :].rearrange("o k e -> (o k) e")).then_inc(s_ea[0], 16)
            for h in range(2):
                sp.wait_ge(s_add[h], NI)
                sp.wait_ge(s_amm[h], NI * GH * GT)
                sp.wait_ge(s_ast[h], 16 * NI)
                sp.wait_ge(s_ew[h], NH + 1)
            sp.wait_ge(s_hotw, NH + 1)
            for k in (1, 2, 3):

                def load(p, cs, nb):
                    for c in cs:
                        sp.wait_ge(S[f"main{c}"], of(k, c, p))
                        if k == 1:
                            sp.wait_ge(s_deg[f"red{c}"], p)
                        nh = nb * P // SN
                        sp.dma_start(at_d_of(c, nh), at_d[bass.ds(2 * CH * p + CH * c, nh), :, :].rearrange("h p n -> p h n")).then_inc(S[f"at{c}"], 16)

                def at_d_of(c, nh):
                    return at[c].rearrange("p (h n) -> p h n", h=CH)[:, 0:nh, :]

                if k == 2:
                    for c in range(2):
                        sp.wait_ge(s_deg[f"red{c}"], NPAIR + 1 - c)
                chunks(sp, load, None)
            for c in range(2):
                sp.wait_ge(S[f"main{c}"], of(4, c, 0))
                sp.wait_ge(s_walk[3][f"st{c}"], 16 * (NT // 2 + (NT % 2) * (1 - c)))
            sp.dma_start(x3b, x3_d.rearrange("(b p) f -> p b f", p=P)).then_inc(s_x3, 16)
            Wk = s_walk[4]

            def store(t, s, p):
                sp.wait_ge(Wk[f"xn{s}"], p + 1)
                if p is NT // 2 and s == 0:
                    sp.dma_start(out_d[t * BT * P:(NB - 1) * P, :].rearrange("(b p) f -> p b f", p=P), xn[s][:, 0:BT - 1, :]).then_inc(Wk[f"st{s}"], 16)
                    sp.dma_start(out_d[(NB - 1) * P:N, :], xn[s][0:LAST, BT - 1, :]).then_inc(Wk[f"st{s}"], 16)
                else:
                    sp.dma_start(out_d[bass.ds(t * (BT * P), BT * P), :].rearrange("(b p) f -> p b f", p=P), xn[s]).then_inc(Wk[f"st{s}"], 16)

            walk(sp, store)
            sp.wait_ge(Wk["st0"], 16 * (NT // 2 + 2))
            sp.wait_ge(Wk["st1"], 16 * (NT // 2))

        @block.gpsimd
        def _(pool):
            nc.gpsimd.memset(edge_w[:, :, :], 0.0).then_inc(s_const, 1)
            nc.gpsimd.memset(ident[:, :], 0.0)
            nc.gpsimd.memset(x[:, NB - 1, :], 0.0).then_inc(s_const, 1)
            pool.wait_ge(s_const, 2)
            nc.gpsimd.affine_select(out=ident[:, :], in_=ident[:, :], compare_op=ALU.not_equal, fill=1.0,
                                    base=0, pattern=[[-1, P]], channel_multiplier=1)
            nc.gpsimd.memset(ones[:, :], 1.0)
            nc.gpsimd.memset(ones16[:, :], 1.0)
            nc.gpsimd.iota(cols_key[:, :], [[1, NB], [NB, GN]], base=0, channel_multiplier=0, allow_small_or_imprecise_dtypes=True)
            nc.gpsimd.iota(cols_p[:, :], [[1, P]], base=0, channel_multiplier=0, allow_small_or_imprecise_dtypes=True)
            nc.gpsimd.iota(cols_pf[:, :], [[1, P]], base=0, channel_multiplier=0, allow_small_or_imprecise_dtypes=True)
            nc.gpsimd.iota(group_dst[:, :], [[P * GN, GC]], base=0, channel_multiplier=GN, allow_small_or_imprecise_dtypes=True)
            nc.gpsimd.memset(eps_ln[:, 0:1], 1.0)
            nc.gpsimd.memset(eps_ln[:, 1:2], 1e-5)
            nc.gpsimd.memset(eps_ln[:, 2:3], 1e-6)
            nc.gpsimd.memset(eps_ln[:, 3:4], 0.0)
            nc.gpsimd.iota(valid[:, :], [[0, 1]], base=0, channel_multiplier=1, allow_small_or_imprecise_dtypes=True)
            nc.gpsimd.iota(group_key[:, :], [[W, G]], base=0, channel_multiplier=0, allow_small_or_imprecise_dtypes=True).then_inc(s_const, 1)
            pool.wait_ge(s_rowst, 16 * NT)
            with pool.Fori(0, NI) as i:
                for h in range(2):
                    pool.wait_ge(s_msg[h], i * 2)
                    pool.wait_ge(s_idx[h], i * 16 + 16)
                    pool.sem_inc(s_seen, 1)
                    for t in range(T8):
                        nc.gpsimd.indirect_dma_start(gath[:, T8 * h + t, :], None, xw_d,
                                                     bass.IndirectOffsetOnAxis(ap=idx[:, h, t:t + 1], axis=0)).then_inc(s_gath[h], 16)
            for k, bias in ((1, B_L1), (2, B_L2), (3, None)):
                Wk = s_walk[k]
                if k == 1:
                    for h in range(2):
                        pool.wait_ge(s_amm[h], NI * GH * GT)

                def residual(t, s, p):
                    pool.wait_ge(Wk[f"xn{s}"], p + 1)
                    if k < 3:
                        nc.gpsimd.tensor_tensor(blocks(y, t), xn[s], vecs[:, bias, :].unsqueeze(1).broadcast_to([P, BT, D]), ALU.add).then_inc(Wk[f"yb{s}"], 1)
                    else:
                        pool.dma_start(x3_d[bass.ds(t * (BT * P), BT * P), :].rearrange("(b p) f -> p b f", p=P), xn[s]).then_inc(Wk[f"st{s}"], 16)

                walk(pool, residual)
            pool.wait_ge(s_x3, 16)
            nc.gpsimd.tensor_tensor(x3b, x3b, vecs[:, BN_BETA, :].unsqueeze(1).broadcast_to([P, NB, D]), ALU.add).then_inc(s_bn_pool, 1)

        @block.vector
        def _(v):
            v.wait_ge(s_in["xT"], 16)
            with v.Fori(0, NT) as i:
                v.wait_ge(s_rowxw, 2 * i)
                nc.vector.tensor_copy(xwS[:, 0:BT, :], yT[:, bass.ds(i * (BT * P), BT * P)].rearrange("p (b n) -> p b n", n=P)).then_inc(s_rowgo, 1)
                for q, nb in ((0, 4), (1, BT - 4)):
                    v.wait_ge(s_rowxw, 2 * i + q + 1)
                    if q == 0:
                        v.wait_ge(s_rowst, 16 * i)
                    nc.vector.tensor_copy(xwS[:, T8 + 4 * q:T8 + 4 * q + nb, :], PB[:, q, 0:nb * P].rearrange("p (b n) -> p b n", n=P)).then_inc(s_rowev, 1)
            v.wait_ge(s_rowev, 2 * NT)
            nc.vector.memset(yT[:, :], 0.0).then_inc(s_zero, 1)
            v.wait_ge(s_in["w"], 32)
            v.wait_ge(s_in["x"], 32)
            nc.vector.tensor_tensor(x[:, :, :], x[:, :, :], vecs[:, B_L0, :].unsqueeze(1).broadcast_to([P, NB, D]), ALU.add).then_inc(s_fin["bias"], 1)
            v.wait_ge(s_in["src"], 16)
            v.wait_ge(s_in["dst"], 16)
            v.wait_ge(s_in["first_b"], 16)
            v.wait_ge(s_const, 3)
            nc.vector.memset(rel[:, T:T + T8], 0.0)
            nc.vector.memset(key[:, T:TT], -1.0)
            nc.vector.memset(src_lo[:, T:TT], -1.0)
            nc.vector.tensor_scalar(src_hi_i, src_i, 7, None, ALU.logical_shift_right).then_inc(s_tab, 1)
            nc.vector.tensor_scalar(less.bitcast(I32), src_i, P - 1, None, ALU.bitwise_and).then_inc(s_tab, 1)
            nc.vector.tensor_copy(first_f, first_i).then_inc(s_tab, 1)
            v.wait_ge(s_tab, 2)
            nc.vector.scalar_tensor_tensor(out=key[:, 0:T], in0=dst_i, scalar=float(NB), in1=src_hi_i, op0=ALU.mult, op1=ALU.add).then_inc(s_tab, 1)
            nc.vector.tensor_copy(src_lo[:, 0:T], less.bitcast(I32)).then_inc(s_tab, 1)
            v.wait_ge(s_in["half_b"], 16)
            nc.vector.tensor_tensor(rel[:, 0:T].rearrange("p (n t) -> p n t", t=T8), half_i.unsqueeze(2).broadcast_to([P, NH, T8]),
                                    dst_i.rearrange("p (n t) -> p n t", t=T8), ALU.subtract).then_inc(s_tab, 1)
            v.wait_ge(s_tab, 6)
            for c in range(GC):
                last = nc.vector.tensor_scalar(less, first_f, group_dst[:, c:c + 1], None, ALU.is_lt, ALU.add, accum_out=start_f[:, c:c + 1])
                if c < GC - 1:
                    last = last.then_inc(s_zero, 1)
                    v.wait_ge(s_zero, c + 2)
            last.then_inc(s_tab, 1)
            v.wait_ge(s_tab, 7)
            nc.vector.tensor_scalar(start_i[:, :], start_f[:, :], -1.0, 0.0, ALU.add, ALU.max).then_inc(s_tab, 1)
            v.wait_ge(s_in["start"], 16)
            v.wait_ge(s_in["first"], 16)

            with v.Fori(0, NI) as i:
                for h in range(2):
                    n = 2 * i + h
                    win_at = v.value_load(win_tab[0:1, bass.ds(i * 2 + h, 1)], min_val=0, max_val=NP)
                    _, first_tile = nc.values_load_multi_w_load_instructions(start_tab[0:1, bass.ds(i * (2 * GH) + GH * h, GH)],
                                                                             engines=DVE_ONLY, min_val=0, max_val=T - 1, skip_runtime_bounds_check_because="a count of tiles, less one")
                    for j in range(GH):
                        nc.vector.tensor_scalar(rel_key[:, GH * h + j, :], key[:, bass.ds(first_tile[j], GT)], group_key[:, bass.ds(i * (2 * GH) + (GH * h + j), 1)],
                                                None, ALU.subtract).then_inc(s_rel[h], 1)
                    v.wait_ge(s_win[h], i)
                    for q in range(2):
                        v.wait_ge(s_ew[q], n + 1)
                        if q == 0:
                            v.wait_ge(s_gath[h], i * (16 * T8) + 16 * T8)
                        b = T8 * h + 4 * q
                        nc.vector.tensor_tensor(msg[:, b:b + 4, :], PB[:, q, :].rearrange("p (t f) -> p t f", f=D), gath[:, b:b + 4, :], ALU.mult).then_inc(s_msg[h], 1)
                    for j in range(GH):
                        v.wait_ge(s_rel[h], i * GH + (j + 1))
                        for k in range(GT):
                            s = GT * j + k
                            if s == 0:
                                v.wait_ge(s_amm[h], i * (GH * GT))
                            nc.vector.tensor_scalar(hot_lo[:, GH * GT * h + s, :], cols_p[:, :], src_lo[:, bass.ds(first_tile[j] + k, 1)], None, ALU.is_equal)
                            nc.vector.tensor_scalar(hot_key[:, GH * GT * h + s, :], cols_key[:, :], rel_key[:, GH * h + j, k:k + 1], None, ALU.is_equal).then_inc(s_hot[h], 1)
                    v.wait_ge(s_win[h], i + 1)
                    v.wait_ge(s_add[1 - h], i + h)
                    where = yT[:, bass.ds(win_at, WIN)]
                    nc.vector.tensor_tensor(where, where, PB[:, 2 + h, 0:WIN], ALU.add).then_inc(s_add[h], 1)

            F = s_fin

            def finish(t, s, p):
                v.wait_ge(F["mm"], t + 1)
                for q, nb in ((0, 4), (1, BT - 4)):
                    here = x[:, bass.ds(t * BT + 4 * q, nb), :]
                    nc.vector.tensor_tensor(here, here, PB[:, q, 0:nb * P].rearrange("p (b f) -> p b f", f=D), ALU.add).then_inc(F["add"], 1)
                v.wait_ge(F["add"], 2 * t + 2)
                v.sem_inc(s_past, 1)
                for b in range(BT):
                    last = nc.vector.bn_stats(stats[:, 0, b, :], x[:, bass.ds(t * BT + b, 1), :].rearrange("p o f -> p (o f)"))
                last.then_inc(F["stats"], 1)
                v.wait_ge(F["stats"], 3 * t + 1)
                v.sem_inc(s_past, 1)
                for b in range(BT):
                    last = nc.vector.bn_aggr(mv_turn[:, 0, b, :], stats[:, 0, b, :])
                last.then_inc(F["stats"], 1)
                v.wait_ge(F["stats"], 3 * t + 2)
                nc.vector.tensor_copy(mean_var[:, bass.ds(t * BT, BT), :], mv_turn[:, 0, :, :]).then_inc(F["stats"], 1)

            v.wait_ge(F["bias"], 1)
            walk(v, finish)

            def norm(k):
                v.wait_ge(s_norm["sqrt"], k)
                nc.vector.reciprocal(rstd[:, :], rstd[:, :]).then_inc(s_norm["recip"], 1)
                v.wait_ge(s_norm["recip"], k)
                nc.vector.scalar_tensor_tensor(out=shift[:, :], in0=mean_var[:, :, 0], scalar=-1.0, in1=rstd[:, :], op0=ALU.mult, op1=ALU.mult).then_inc(s_norm["ready"], 1)

            for k in (1, 2, 3):
                norm(k)
                Wk = s_walk[k]

                def split(t, s, p):
                    v.wait_ge(Wk[f"xn{s}"], p + 1)
                    v.wait_ge(Wk[f"hi{s}"], p)
                    if k == 1:
                        nc.vector.tensor_scalar(xs[s], xn[s], SCALE, None, ALU.mult).then_inc(Wk[f"xs{s}"], 1)
                    else:
                        nc.vector.tensor_tensor(xs[s], xn[s], SRC_SCALE[k][:, bass.ds(t * BT, BT)].unsqueeze(2).broadcast_to([P, BT, D]), ALU.mult).then_inc(Wk[f"xs{s}"], 1)
                    v.wait_ge(Wk[f"hi{s}"], p + 1)
                    nc.vector.tensor_tensor(blocks(parts_v[1], t), xs[s], blocks(parts_v[0], t), ALU.subtract).then_inc(Wk["lo"], 1)
                    if k == 1:
                        v.wait_ge(Wk["lin"], t + 1)
                        v.wait_ge(Wk[f"yb{s}"], p + 1)
                        for q, nb in ((0, 4), (1, BT - 4)):
                            here = y[:, bass.ds(t * BT + 4 * q, nb), :]
                            nc.vector.tensor_tensor(here, here, PB[:, 4 + q, 0:nb * P].rearrange("p (b f) -> p b f", f=D), ALU.add).then_inc(Wk["y"], 1)
                    if k == 3:
                        v.wait_ge(Wk["lin"], t + 1)
                        for q, nb in ((0, 4), (1, BT - 4)):
                            nc.vector.tensor_tensor(x[:, bass.ds(t * BT + 4 * q, nb), :], PB[:, 4 + q, 0:nb * P].rearrange("p (b f) -> p b f", f=D),
                                                    vecs[:, B_LIN, :].unsqueeze(1).broadcast_to([P, nb, D]), ALU.add)
                            for b in range(4 * q, 4 * q + nb):
                                last = nc.vector.scalar_tensor_tensor(out=y[:, bass.ds(t * BT + b, 1), :].rearrange("p o f -> p (o f)"), in0=PB[:, 6 + q, (b - 4 * q) * P:(b - 4 * q + 1) * P],
                                                                      scalar=self_l3[:, bass.ds(t * BT + b, 1)], in1=vecs[:, B_GCN, :], op0=ALU.mult, op1=ALU.add)
                            last.then_inc(Wk["y"], 1)

                walk(v, split)

                def dense(p, cs, nb):
                    at_block = [CB * (2 * p + c) for c in range(2)]
                    if k == 1:
                        for c in cs:
                            v.wait_ge(S[f"at{c}"], 16 * of(k, c, p + 1))
                            nc.vector.tensor_reduce(out=sdeg_part[:, bass.ds(2 * p + c, 1), :].rearrange("p o b -> p (o b)"),
                                                    in_=at_v[c][:, 0:nb * P // SN, :, :].rearrange("p c h d -> p h c d"), axis=AX.XY, op=ALU.add).then_inc(s_deg[f"red{c}"], 1)
                        for c in cs:
                            here = [a[:, bass.ds(at_block[c], nb)] for a in (deg, scale_l1)]
                            v.wait_ge(s_deg[f"mm{c}"], 2 * p + 2)
                            nc.vector.tensor_copy(here[0], PB[:, 6 + c, 0:nb]).then_inc(s_deg[f"col{c}"], 1)
                            v.wait_ge(s_deg[f"col{c}"], 3 * p + 1)
                            nc.vector.tensor_scalar(here[1], here[0], 1.0, SCALE, ALU.max, ALU.mult).then_inc(s_deg[f"col{c}"], 1)
                            v.wait_ge(s_deg[f"col{c}"], 3 * p + 2)
                            v.sem_inc(s_past, 1)
                            nc.vector.reciprocal(here[1], here[1]).then_inc(s_deg[f"col{c}"], 1)
                    for c in cs:
                        v.wait_ge(S[f"lin{c}"], of(k, c, p + 1))
                        if k == 1:
                            v.wait_ge(s_deg[f"col{c}"], 3 * p + 3)
                        if k == 3:
                            v.wait_ge(s_gated[f"zt{c}"], p)
                            v.wait_ge(s_gated[f"mix{c}"], 4 * p)
                        for b in range(nb):
                            row = y[:, bass.ds(at_block[c] + b, 1), :].rearrange("p o f -> p (o f)")
                            last = nc.vector.scalar_tensor_tensor(out=zpre[c][:, b * P:b * P + P] if k == 3 else row, in0=PB[:, 4 + c, b * P:b * P + P],
                                                                  scalar=DST_SCALE[k][:, bass.ds(at_block[c] + b, 1)], in1=row, op0=ALU.mult, op1=ALU.add)
                        last.then_inc(S[f"y{c}"], 1)
                    for c in cs:
                        if k < 3:
                            v.wait_ge(S[f"y{c}"], of(k, c, p + 1))
                            v.sem_inc(s_past, 1)
                            for b in range(nb):
                                last = nc.vector.bn_stats(stats[:, c, b, :], y[:, bass.ds(at_block[c] + b, 1), :].rearrange("p o f -> p (o f)"))
                            last.then_inc(S[f"stats{c}"], 1)
                            v.wait_ge(S[f"stats{c}"], 3 * of(k, c, p) + 1)
                            v.sem_inc(s_past, 1)
                            for b in range(nb):
                                last = nc.vector.bn_aggr(mv_turn[:, c, b, :], stats[:, c, b, :])
                            last.then_inc(S[f"stats{c}"], 1)
                            v.wait_ge(S[f"stats{c}"], 3 * of(k, c, p) + 2)
                            nc.vector.tensor_copy(mean_var[:, bass.ds(at_block[c], nb), :], mv_turn[:, c, 0:nb, :]).then_inc(S[f"stats{c}"], 1)
                        else:
                            n = nb * P
                            xl = x[:, bass.ds(at_block[c], nb), :].rearrange("p b f -> p (b f)")
                            v.wait_ge(s_gated[f"z{c}"], p + 1)
                            v.wait_ge(s_gated[f"zt{c}"], p + 1)
                            nc.vector.tensor_tensor(zpre[c][:, 0:n], zpre[c][:, 0:n], xl, ALU.subtract).then_inc(s_gated[f"mix{c}"], 1)
                            v.wait_ge(s_gated[f"mix{c}"], 4 * p + 1)
                            v.wait_ge(s_gated[f"g{c}"], p + 1)
                            nc.vector.tensor_tensor(zpre[c][:, 0:n], zpre[c][:, 0:n], gate[c][:, 0:n], ALU.mult).then_inc(s_gated[f"mix{c}"], 1)
                            v.wait_ge(s_gated[f"mix{c}"], 4 * p + 2)
                            nc.vector.tensor_tensor(zpre[c][:, 0:n], zpre[c][:, 0:n], xl, ALU.add).then_inc(s_gated[f"mix{c}"], 1)
                            v.wait_ge(s_gated[f"mix{c}"], 4 * p + 3)
                            nc.vector.tensor_scalar(xl, zpre[c][:, 0:n], 0.0, None, ALU.max).then_inc(s_gated[f"mix{c}"], 1)

                chunks(v, dense, None)
                if k == 1:
                    for c in range(2):
                        v.wait_ge(s_deg[f"red{c}"], NPAIR + 1 - c)
                        v.wait_ge(s_deg[f"col{c}"], 3 * (NPAIR + 1 - c))
                    nc.vector.tensor_reduce(out=sdeg, in_=sdeg_part[:, :, :].rearrange("p c b -> p b c"), axis=AX.X, op=ALU.add).then_inc(s_root, 1)
                    v.wait_ge(s_root, 1)
                    nc.vector.tensor_scalar(roots[:, 0, :], sdeg, 1.0, 1e-6, ALU.max, ALU.add).then_inc(s_root, 1)
                    nc.vector.tensor_scalar(roots[:, 1, :], deg, 1e-6, None, ALU.add).then_inc(s_root, 1)
                    nc.vector.tensor_scalar(roots[:, 2, :], deg, 1.0, 1e-12, ALU.add, ALU.max).then_inc(s_root, 1)
                    v.wait_ge(s_root, 5)
                    nc.vector.reciprocal(roots, roots).then_inc(s_root, 1)
                    v.wait_ge(s_root, 6)
                    nc.vector.tensor_scalar(src_l2, roots[:, 0, :], SCALE, None, ALU.mult).then_inc(s_root, 1)
                    nc.vector.tensor_scalar(dst_l2, roots[:, 1, :], 1 / SCALE, None, ALU.mult).then_inc(s_root, 1)
                    nc.vector.tensor_scalar(src_l3, roots[:, 2, :], SCALE, None, ALU.mult).then_inc(s_root, 1)
                    nc.vector.tensor_scalar(dst_l3, roots[:, 2, :], 1 / SCALE, None, ALU.mult).then_inc(s_root, 1)
                    nc.vector.tensor_tensor(self_l3, roots[:, 2, :], roots[:, 2, :], ALU.mult).then_inc(s_root, 1)
                    v.wait_ge(s_root, 11)

            step = [0]

            def bn(instruction):
                instruction.then_inc(s_bn, 1)
                step[0] += 1

            for c in range(2):
                v.wait_ge(s_gated[f"mix{c}"], 4 * (NPAIR + 1 - c))
            bn(nc.vector.tensor_scalar(valid[:, :], valid[:, :], float(LAST), None, ALU.is_lt))
            v.wait_ge(s_bn, 1)
            bn(nc.vector.tensor_scalar(x[:, NB - 1, :], x[:, NB - 1, :], valid[:, :], None, ALU.mult))
            v.wait_ge(s_bn, 2)
            bn(nc.vector.tensor_reduce(out=bn_row[:, 0, :], in_=x[:, :, :].rearrange("p b f -> p f b"), axis=AX.X, op=ALU.add))
            v.wait_ge(s_bn_pe, 1)
            bn(nc.vector.tensor_scalar(bn_row[:, 1, :], PB[:, 0, 0:D], 1.0 / N, None, ALU.mult))
            v.wait_ge(s_bn, 4)
            bn(nc.vector.tensor_tensor(y[:, :, :], x[:, :, :], bn_row[:, 1, :].unsqueeze(1).broadcast_to([P, NB, D]), ALU.subtract))
            v.wait_ge(s_bn, 5)
            bn(nc.vector.tensor_scalar(y[:, NB - 1, :], y[:, NB - 1, :], valid[:, :], None, ALU.mult))
            v.wait_ge(s_bn_act, 1)
            bn(nc.vector.tensor_reduce(out=bn_row[:, 2, :], in_=sq.rearrange("p b f -> p f b"), axis=AX.X, op=ALU.add))
            v.wait_ge(s_bn_act, 2)
            bn(nc.vector.reciprocal(bn_row[:, 3, :], bn_row[:, 3, :]))
            v.wait_ge(s_bn, 8)
            bn(nc.vector.tensor_tensor(bn_row[:, 3, :], bn_row[:, 3, :], vecs[:, BN_GAMMA, :], ALU.mult))
            v.wait_ge(s_bn, 9)
            bn(nc.vector.tensor_tensor(y[:, :, :], y[:, :, :], bn_row[:, 3, :].unsqueeze(1).broadcast_to([P, NB, D]), ALU.mult))
            v.wait_ge(s_bn, 10)
            v.wait_ge(s_bn_pool, 1)
            bn(nc.vector.tensor_tensor(y[:, :, :], y[:, :, :], x3b, ALU.add))
            v.wait_ge(s_bn, 11)
            for b0 in range(0, NB, BT):
                for b in range(BT):
                    last = nc.vector.bn_stats(stats[:, b0 // BT % 2, b, :], y[:, b0 + b, :])
                bn(last)
                v.wait_ge(s_bn, step[0])
                for b in range(BT):
                    last = nc.vector.bn_aggr(mean_var[:, b0 + b, :], stats[:, b0 // BT % 2, b, :])
            bn(last)
            norm(4)

        @block.tensor
        def _(pe):
            pe.wait_ge(s_in["w"], 32)
            pe.wait_ge(s_in["edge_w"], 16 * T8)
            with pe.Fori(0, NT) as i:
                pe.wait_ge(s_rowgo, i + 1)
                for b in range(BT):
                    if b % 4 == 0:
                        pe.wait_ge(s_rowev, 2 * i + b // 4)
                    last = nc.tensor.matmul(PB[:, b // 4, b % 4 * P:b % 4 * P + P], xwS[:, b, :], wts[:, 0, :], start=True, stop=True)
                    if b in (3, BT - 1):
                        last.then_inc(s_rowxw, 1)

            def edge_products(h, n):
                for q in range(2):
                    nc.tensor.matmul(PB[:, q, :], ea[:, h, :], edge_w[:, 4 * q:4 * q + 4, :], start=True, stop=True).then_inc(s_ew[q], 1)

            pe.wait_ge(s_rowev, 2 * NT)
            pe.wait_ge(s_ea[0], 16)
            edge_products(0, 0)
            with pe.Fori(0, NI) as i:
                for h in range(2):
                    n = 2 * i + h
                    for j in range(GH):
                        if j == 0:
                            pe.wait_ge(s_msg[h], i * 2 + 2)
                            pe.wait_ge(s_hotw, n + 1)
                            pe.wait_ge(s_add[h], i)
                            for t in range(T8):
                                last = nc.tensor.matmul(PB[:, 2 + h, 0:WIN], msg[:, T8 * h + t, :], hot_win[:, T8 * h + t, :], start=(t == 0), stop=(t == T8 - 1))
                            last.then_inc(s_win[h], 1)
                            pe.wait_ge(s_ea[1 - h], i * 16 + 16 * (1 + h))
                            edge_products(1 - h, n + 1)
                        pe.wait_ge(s_aev[j], n)
                        for k in range(GT):
                            s = GT * j + k
                            pe.wait_ge(s_hot[h], i * (GH * GT) + (s + 1))
                            nc.tensor.matmul(PB[:, 4 + j, 0:W], hot_lo[:, GH * GT * h + s, :], hot_key[:, GH * GT * h + s, :],
                                             start=(k == 0), stop=(k == GT - 1)).then_inc(s_amm[h], 1)

            def turn(t, s, p):
                pe.wait_ge(s_fin["stage"], t + 1)
                pe.wait_ge(s_fin["add"], 2 * t)
                for b in range(BT):
                    last = nc.tensor.transpose(PB[:, b // 4, b % 4 * P:b % 4 * P + P], xs[0][:, b, :], ident[:, :])
                last.then_inc(s_fin["mm"], 1)

            walk(pe, turn)
            for k in (1, 2, 3):
                Wk = s_walk[k]

                def linear(t, s, p):
                    pe.wait_ge(Wk[f"xn{s}"], p + 1)
                    pe.wait_ge(Wk["xnT"], t)
                    for b in range(BT):
                        last = nc.tensor.transpose(PB[:, 2 + b // 4, b % 4 * P:b % 4 * P + P], xn[s][:, b, :], ident[:, :])
                    last.then_inc(Wk[f"tp{s}"], 1)
                    pe.wait_ge(Wk["xnT"], t + 1)
                    pe.wait_ge(Wk["y"], 2 * t)
                    for b in range(BT):
                        for bank, w in ((4, W_R1),) if k == 1 else ((4, W_LIN), (6, W_GCN)):
                            last = nc.tensor.matmul(PB[:, bank + b // 4, b % 4 * P:b % 4 * P + P], xnT[:, b, :], wts[:, w, :], start=True, stop=True)
                    last.then_inc(Wk["lin"], 1)

                if k != 2:
                    walk(pe, linear)
                pe.wait_ge(Wk["lo"], NT)
                if k != 2:
                    pe.wait_ge(Wk["y"], 2 * NT)

                def dense(p, cs, nb):
                    n = nb * P
                    for c in cs:
                        pe.wait_ge(S[f"at{c}"], 16 * of(k, c, p + 1))
                        pe.wait_ge(S[f"evac{c}"], of(k, c, p))
                        if k == 1:
                            pe.wait_ge(s_deg[f"row{c}"], p)
                        for b in range(NB):
                            piece = at_v[c][:, 0:n // SN, b, :]
                            nc.tensor.matmul(PB[:, c, 0:n], parts_v[0][:, b, :], piece, start=(b == 0), stop=False)
                            if k == 1:
                                last = nc.tensor.matmul(PB[:, 2 + c, 0:n], ones16[:, :], piece, start=(b == 0), stop=(b == NB - 1))
                                if b == NB - 1:
                                    last.then_inc(s_deg[f"mm{c}"], 1)
                            last = nc.tensor.matmul(PB[:, c, 0:n], parts_v[1][:, b, :], piece, start=False, stop=(b == NB - 1))
                        last.then_inc(S[f"main{c}"], 1)
                    for c in cs:
                        pe.wait_ge(S[f"evac{c}"], of(k, c, p + 1))
                        pe.wait_ge(S[f"y{c}"], of(k, c, p))
                        for b in range(nb):
                            last = nc.tensor.matmul(PB[:, 4 + c, b * P:b * P + P], aggT[c][:, b * P:b * P + P], wts[:, WGT[k], :], start=True, stop=True)
                        last.then_inc(S[f"lin{c}"], 1)
                        if k == 1:
                            pe.wait_ge(s_deg[f"row{c}"], p + 1)
                            pe.wait_ge(s_deg[f"col{c}"], 3 * p)
                            for b in range(nb):
                                last = nc.tensor.matmul(PB[:, 6 + c, b:b + 1], deg_row[0:1, c, b * P:b * P + P], ones[0:1, 0:1], start=True, stop=True)
                            last.then_inc(s_deg[f"mm{c}"], 1)
                    if k == 3:
                        for c in cs:
                            pe.wait_ge(s_gated[f"z{c}"], p + 1)
                            pe.wait_ge(s_gated[f"zts{c}"], p)
                            for b in range(nb):
                                last = nc.tensor.transpose(PB[:, 2 + c, b * P:b * P + P], zpre[c][:, b * P:b * P + P], ident[:, :])
                            last.then_inc(s_gated[f"zt{c}"], 1)
                        for c in cs:
                            pe.wait_ge(s_gated[f"g{c}"], p)
                            for b in range(nb):
                                nc.tensor.matmul(PB[:, 6 + c, b * P:b * P + P], ident[:, :], vecs[:, B_GATE, :], start=True, stop=False)
                                if b == 0:
                                    pe.wait_ge(s_gated[f"zts{c}"], p + 1)
                                last = nc.tensor.matmul(PB[:, 6 + c, b * P:b * P + P], zT[c][:, b * P:b * P + P], wts[:, W_GATE, :], start=False, stop=True)
                            last.then_inc(s_gated[f"gate{c}"], 1)

                chunks(pe, dense, None)
            pe.wait_ge(s_bn, 3)
            nc.tensor.matmul(PB[:, 0, 0:D], ones[:, :], bn_row[:, 0, :], start=True, stop=True).then_inc(s_bn_pe, 1)
            pe.wait_ge(s_bn, 7)
            nc.tensor.matmul(PB[:, 1, 0:D], ones[:, :], bn_row[:, 2, :], start=True, stop=True).then_inc(s_bn_pe, 1)

        @block.scalar
        def _(act):
            act.wait_ge(s_tab, 8)
            def one_hot_window(h, base, n):
                for t in range(T8):
                    last = nc.scalar.activation(dist[:, T8 * h + t, :], cols_pf[:, 0:WIN], ACT.Abs, bias=rel[:, bass.ds(base + t, 1)])
                last.then_inc(s_dist, 1)
                act.wait_ge(s_dist, n + 1)
                nc.scalar.activation(hot_win[:, T8 * h:T8 * h + T8, :], dist[:, T8 * h:T8 * h + T8, :], ACT.Relu, scale=-1.0, bias=eps_ln[:, 0:1]).then_inc(s_hotw, 1)

            one_hot_window(0, 0, 0)
            with act.Fori(0, NI) as i:
                for h in range(2):
                    act.wait_ge(s_ast[h], i * 16)
                    for j in range(GH):
                        if j == 0:
                            act.wait_ge(s_win[1 - h], i + h)
                            one_hot_window(1 - h, i * (2 * T8) + T8 * (h + 1), 2 * i + (h + 1))
                        act.wait_ge(s_amm[h], i * (GH * GT) + GT * (j + 1))
                        nc.scalar.copy(stage[:, h, :].rearrange("p (b d) -> p b d", d=SN)[:, :, GN * j:GN * j + GN],
                                       PB[:, 4 + j, 0:W].rearrange("p (b d) -> p b d", d=GN)).then_inc(s_aev[j], 1)
                    act.wait_ge(s_aev[GH - 1], 2 * i + h + 1)
                    act.dma_start(at_d[bass.ds(2 * i + h, 1), :, :].rearrange("o p n -> (o p) n"), stage[:, h, :]).then_inc(s_ast[h], 16)

            for h in range(2):
                act.wait_ge(s_add[h], NI)
                act.wait_ge(s_ast[h], 16 * NI)

            def stage_sum(t, s, p):
                act.wait_ge(s_fin["mm"], t)
                nc.scalar.copy(xs[0], yT[:, bass.ds(t * (BT * P), BT * P)].rearrange("p (b n) -> p b n", n=P)).then_inc(s_fin["stage"], 1)

            walk(act, stage_sum)

            def norm(k):
                if k == 1:
                    act.wait_ge(s_fin["stats"], 3 * NT)
                elif k == 4:
                    act.wait_ge(s_bn, 11 + NT + 1)
                else:
                    for c in range(2):
                        act.wait_ge(S[f"stats{c}"], 3 * of(k, c, 0))
                nc.scalar.activation(rstd[:, :], mean_var[:, :, 1], ACT.Sqrt, bias=eps_ln[:, 1:2]).then_inc(s_norm["sqrt"], 1)

            def rows(k, t, s, p):
                Wk = s_walk[k]
                for n in {1: ("tp", "xs", "yb"), 2: ("xs", "yb"), 3: ("tp", "xs"), 4: ()}[k]:
                    act.wait_ge(Wk[f"{n}{s}"], p)
                if k >= 3:
                    act.wait_ge(Wk[f"st{s}"], 16 * p)
                for b in range(BT):
                    last = nc.scalar.activation(xn[s][:, b, :], BN_SRC[k][:, bass.ds(t * BT + b, 1), :].rearrange("p o f -> p (o f)"), ACT.Identity,
                                                scale=rstd[:, bass.ds(t * BT + b, 1)], bias=shift[:, bass.ds(t * BT + b, 1)])
                last.then_inc(Wk[f"xn{s}"], 1)

            for k in (1, 2, 3):
                Wk = s_walk[k]
                norm(k)
                act.wait_ge(s_norm["ready"], k)

                def split(t, s, p):
                    rows(k, t, s, p)
                    act.wait_ge(Wk[f"xs{s}"], p + 1)
                    nc.scalar.copy(blocks(parts_v[0], t), xs[s]).then_inc(Wk[f"hi{s}"], 1)
                    if k != 2:
                        act.wait_ge(Wk[f"tp{s}"], p + 1)
                        act.wait_ge(Wk["lin"], t)
                        for q, nb in ((0, 4), (1, BT - 4)):
                            last = nc.scalar.copy(xnT[:, 4 * q:4 * q + nb, :], PB[:, 2 + q, 0:nb * P].rearrange("p (b f) -> p b f", f=D))
                        last.then_inc(Wk["xnT"], 1)

                walk(act, split)
                act.wait_ge(Wk["lo"], NT)
                for s in range(2):
                    if k < 3:
                        act.wait_ge(Wk[f"yb{s}"], NT // 2 + 1 - s)
                    else:
                        act.wait_ge(Wk[f"st{s}"], 16 * (NT // 2 + 1 - s))

                def dense(p, cs, nb):
                    n = nb * P
                    for c in cs:
                        act.wait_ge(S[f"main{c}"], of(k, c, p + 1))
                        act.wait_ge(S[f"lin{c}"], of(k, c, p))
                        nc.scalar.copy(aggT[c][:, 0:n], PB[:, c, 0:n]).then_inc(S[f"evac{c}"], 1)
                        if k == 1:
                            act.wait_ge(s_deg[f"mm{c}"], 2 * p + 1)
                            nc.scalar.copy(deg_row[0:1, c, 0:n], PB[0:1, 2 + c, 0:n]).then_inc(s_deg[f"row{c}"], 1)
                    if k == 3:
                        for c in cs:
                            act.wait_ge(S[f"y{c}"], of(k, c, p + 1))
                            nc.scalar.activation(zpre[c][:, 0:n], zpre[c][:, 0:n], ACT.Tanh).then_inc(s_gated[f"z{c}"], 1)
                        for c in cs:
                            act.wait_ge(s_gated[f"zt{c}"], p + 1)
                            act.wait_ge(s_gated[f"gate{c}"], p)
                            nc.scalar.copy(zT[c][:, 0:n], PB[:, 2 + c, 0:n]).then_inc(s_gated[f"zts{c}"], 1)
                        for c in cs:
                            act.wait_ge(s_gated[f"gate{c}"], p + 1)
                            act.wait_ge(s_gated[f"mix{c}"], 4 * p)
                            nc.scalar.activation(gate[c][:, 0:n], PB[:, 6 + c, 0:n], ACT.Sigmoid).then_inc(s_gated[f"g{c}"], 1)

                chunks(act, dense, None)
                if k == 1:
                    act.wait_ge(s_root, 4)
                    nc.scalar.activation(roots, roots, ACT.Sqrt).then_inc(s_root, 1)
            act.wait_ge(s_bn, 6)
            nc.scalar.activation(sq, y[:, :, :], ACT.Square).then_inc(s_bn_act, 1)
            act.wait_ge(s_bn_pe, 2)
            nc.scalar.activation(bn_row[:, 3, :], PB[:, 1, 0:D], ACT.Sqrt, scale=1.0 / N, bias=eps_ln[:, 1:2]).then_inc(s_bn_act, 1)
            norm(4)
            act.wait_ge(s_norm["ready"], 4)
            walk(act, lambda t, s, p: rows(4, t, s, p))


def layout(a):
    import numpy as np

    x = np.asarray(a["x"])
    xT = np.zeros((D, NP), np.float32)
    xT[:, :N] = x.T
    src = np.zeros(T * P, np.int32)
    src[:E] = a["src"]
    dst = np.full(T * P, NP, np.int32)
    dst[:E] = a["dst"]
    ea = np.zeros(((NH + 1) * T8 * P, ED), np.float32)
    ea[:E] = a["edge_attr_16"]
    w = np.zeros((8, D, D), np.float32)
    w[0] = a["L0_gnn_W"]
    w[1] = np.asarray(a["L1_gnn_W_l"]).T
    w[2] = np.asarray(a["L1_gnn_W_r"]).T
    w[3] = a["L2_gnn_weight"]
    w[4] = a["L3_gnn_gcn_w"]
    w[5] = a["L3_gnn_lin_w"]
    w[6] = a["L3_gnn_gate_w"]
    w[7, :ED] = a["L0_gnn_edge_w"]
    vec = np.stack([np.asarray(a[n]) for n in ("L0_gnn_b", "L1_gnn_b_l", "L2_gnn_bias", "L3_gnn_gcn_b", "L3_gnn_lin_b",
                                               "L3_gnn_gate_b", "L3_gnn_bn_gamma", "L3_gnn_bn_beta")])[None]
    return {
        "in_xT": xT,
        "in_x": np.ascontiguousarray(x),
        "in_ea": np.ascontiguousarray(ea.reshape(NH + 1, T8, P, ED).transpose(0, 1, 3, 2).reshape(NH + 1, T8 * ED, P)),
        "in_idx": np.ascontiguousarray(src.reshape(NH, T8, P).transpose(0, 2, 1)),
        "in_src": np.ascontiguousarray(src.reshape(T, P).T),
        "in_dst": np.ascontiguousarray(dst.reshape(T, P).T),
        "in_first": np.ascontiguousarray(dst.reshape(T, P)[:, 0][None]),
        "in_half": np.ascontiguousarray(dst.reshape(NH, T8 * P)[:, 0][None]),
        "in_w": w,
        "in_vec": np.ascontiguousarray(vec),
    }


def kernel(**inputs):
    import concourse.bacc as bacc
    from concourse.bass_utils import run_bass_kernel_spmd

    arrays = layout(inputs)
    nc = bacc.Bacc("TRN2", target_bir_lowering=False, num_devices=1)
    ins = [nc.dram_tensor(n, a.shape, mybir.dt.from_np(a.dtype), kind="ExternalInput").ap() for n, a in arrays.items()]
    out = nc.dram_tensor("out", (N, D), F32, kind="ExternalOutput").ap()
    build(nc, *ins, out)
    r = run_bass_kernel_spmd(nc, [arrays], core_ids=[0])
    return r.results[0]["out"]
```

```python
from contextlib import ExitStack

import concourse.bass as bass
from concourse import mybir

F32 = mybir.dt.float32
F16 = mybir.dt.float16
I32 = mybir.dt.int32
ALU = mybir.AluOpType
ACT = mybir.ActivationFunctionType
AX = mybir.AxisListType

N = 6250
E = 206250
D = 128
ED = 16
P = 128
NB = -(-N // P)
NP = NB * P
T8 = 8
SN = 32
NH = 2 * max(-(-E // (2 * T8 * P)), NP // (2 * SN) + 1)
NI = NH // 2
T = NH * T8
GN = 8
GH = SN // GN
GT = 4
G = (NH + 1) * GH
GC = -(-(G + 1) // P)
W = GN * NB
TT = T + GT
WIN = 128
YW = NP + WIN
BT = 7
NT = NB // BT
CH = 16
CN = CH * SN
NPAIR = NP // (2 * CN)
TAIL = NP - 2 * NPAIR * CN
SCALE = 1024.0
LAST = N - (NB - 1) * P
NCH = 2 * NPAIR + 1
SB = NB * 3 // 8
XT_CUT = NT // 2 + 1
CB = CN // P
TURNS = [(NT + 1 - s) // 2 for s in range(2)]
(W_L0, W_L1, W_R1, W_L2, W_GCN, W_LIN, W_GATE) = range(7)
(B_L0, B_L1, B_L2, B_GCN, B_LIN, B_GATE, BN_GAMMA, BN_BETA) = range(8)


def build(nc, xT_d, x_d, ea_d, idx_d, src_d, dst_d, next_d, first_d, half_d, w_d, vec_d, out_d):
    DVE_ONLY, ACT_ONLY = [mybir.EngineType.DVE], [mybir.EngineType.Activation]
    ctx = ExitStack()
    with ctx:
        def sb(name, shape, dt=F32):
            return ctx.enter_context(nc.sbuf_tensor(name, shape, dt))

        def sem(name):
            return ctx.enter_context(nc.semaphore(name))

        xw_d = nc.dram_tensor("xw", [NP, D], F32, kind="Internal").ap()
        at_d = nc.dram_tensor("at", [NH, P, NB * SN], F16, kind="Internal").ap()
        x3_d = nc.dram_tensor("x3", [NP, D], F32, kind="Internal").ap()
        start_d = nc.dram_tensor("group_start", [GC, P], I32, kind="Internal").ap()

        x = sb("x", [P, NB, D])
        y = sb("y", [P, NB, D])
        ident = sb("ident", [P, P])
        ones = sb("ones", [P, P])
        ones16 = sb("ones16", [P, P], F16)
        wts = sb("wts", [P, 7, D])
        vecs = sb("vecs", [P, 8, D])
        BIG = sb("big", [P, 2 * CH * NB * SN], F16)
        big_at = [0]

        def part(shape, dt):
            n = 1
            for s in shape[1:]:
                n *= s
            size = n * (2 if dt == F32 or dt == I32 else 1)
            a = BIG[0:shape[0], big_at[0]:big_at[0] + size]
            big_at[0] += size
            if dt != F16:
                a = a.bitcast(dt)
            if len(shape) == 3:
                a = a.rearrange("p (a b) -> p a b", b=shape[2])
            return a

        gath = part([P, 2 * T8, D], F32)
        msg = part([P, 2 * T8, D], F32)
        hot_win = part([P, 2 * T8, WIN], F32)
        dist = part([P, 2 * T8, WIN], F32)
        edge_w = part([P, T8, D], F32)
        ea = part([P, 2, P], F32)
        key = part([P, TT], F32)
        src_lo = part([P, TT], F32)
        rel = part([P, T + T8], F32)
        half_i = part([P, NH], I32)
        deg_at = big_at[0]
        src_i = part([P, T], I32)
        src_hi_i = msg.rearrange("p t f -> p (t f)")[:, 0:T].bitcast(I32)
        dst_i = part([P, T], I32)
        first_i = part([P, T], I32)
        first_f = part([P, T], F32)
        deg_row = BIG[0:1, deg_at:deg_at + 2 * NH * SN].bitcast(F32)
        assert deg_at + 2 * NH * SN <= big_at[0]
        win_tab = part([1, NH], I32)
        neg_group_key = part([P, G], F32)
        hot_lo = part([P, 2 * GH * GT, P], F16)
        start_tab = part([1, GC * P], I32)
        assert big_at[0] <= 2 * CH * NB * SN, big_at[0]
        at = [BIG[:, 0:CH * NB * SN], BIG[:, CH * NB * SN:]]

        yT = sb("yT", [P, YW])
        parts = yT[:, 0:NP].bitcast(F16).rearrange("p (s b f) -> p s b f", s=2, f=D)
        hot_key = y[:, :, :].rearrange("p b f -> p (b f)").bitcast(F16)[:, 0:2 * GH * GT * W].rearrange("p (s f) -> p s f", f=W)
        tmp = sb("tmp", [P, 5, BT * D])
        stage = tmp[:, 0:4, :].rearrange("p a b -> p (a b)")[:, 0:NB * SN].bitcast(F16).rearrange("p (h n) -> p h n", h=2)
        flat = tmp[:, :, :].rearrange("p a b -> p (a b)")
        xn = [tmp[:, k, :].rearrange("p (b f) -> p b f", f=D) for k in (0, 1)]
        xs = [tmp[:, k, :].rearrange("p (b f) -> p b f", f=D) for k in (2, 3)]
        xnT = tmp[:, 4, :].rearrange("p (b f) -> p b f", f=D)
        aggT, zpre, zT, gate = ([flat[:, (2 * k + c) * CN:(2 * k + c + 1) * CN] for c in range(2)] for k in range(4))
        waste = flat[:, 6 * CN:8 * CN].bitcast(F16).rearrange("p (c s n) -> p c s n", c=2, s=2)
        bn_row = flat[:, 0:4 * D].rearrange("p (k f) -> p k f", f=D)
        less = hot_win.rearrange("p t f -> p (t f)")[:, 0:T]
        sdeg_part = sb("sdeg_part", [P, NCH + 2, NB])
        g_deg = sdeg_part[:, NCH:NCH + 2, :]
        small = sb("small", [P, 11, NB])
        deg, sdeg, scale_l1, src_l2, dst_l2, src_l3, dst_l3, self_l3 = (small[:, k, :] for k in range(8))
        roots = small[:, 8:11, :]
        stats = sb("stats", [P, 2, BT, 6])
        mv_turn = sb("mv_turn", [P, 2, BT, 2])
        mean_var = sb("mean_var", [P, NB, 2])
        rstd = sb("rstd", [P, NB])
        shift = sb("shift", [P, NB])
        bias_l0 = sb("bias_l0", [P, 1])
        eps_ln = sb("eps_ln", [P, 4])
        valid = sb("valid", [P, 1])
        idx = sb("idx", [P, 2, T8], I32)
        start_i = sb("start_i", [P, GC], I32)
        start_f = sb("start_f", [P, GC])
        group_dst = sb("group_dst", [P, GC])
        rel_key = sb("rel_key", [P, 2 * GH, GT])
        cols_key = sb("cols_key", [P, W], F16)
        cols_p = sb("cols_p", [P, P], F16)
        cols_pf = sb("cols_pf", [P, P])

        win_cols = sb("win_cols", [P, WIN])
        flags = sb("flags", [P, 3])
        off_f = sb("off_f", [P, 1])
        off_i = sb("off_i", [P, 1], I32)
        rows_d = nc.dram_tensor("rows", [NP, 2 * D], F16, kind="Internal").ap()
        g_src = sb("g_src", [P, T8], I32)
        g_dst = sb("g_dst", [P, T8], I32)
        g_place = sb("g_place", [P, 2, T8])
        g_pad = sb("g_pad", [P, T8])
        next_i = dist.rearrange("p t f -> p (t f)")[:, 0:T].bitcast(I32)
        g_rows = [gath[:, 0:T8, :]] + 3 * [gath[:, 0:T8, :].rearrange("p t f -> p (t f)").bitcast(F16).rearrange("p (t f) -> p t f", f=2 * D)]
        g_hot = [hot_win[:, 0:T8, :]] + 3 * [hot_win[:, 0:T8 // 2, :].rearrange("p t f -> p (t f)").bitcast(F16).rearrange("p (t f) -> p t f", f=P)]
        g_hot_src = dist[:, 0:T8, :]
        g_sum = at[1].bitcast(F32)[:, 0:NP]
        g_block = msg[:, 0, :]

        PB = ctx.enter_context(nc.psum_tensor("pb", [P, 8, 512], F32))

        s_in = {n: sem("in_" + n) for n in ("w", "edge_w", "xT0", "xT1", "vecs", "edges", "firsts", "rows", "x", "start")}
        s_const = sem("consts_made")
        s_rowxw, s_rowev = sem("xw_mm"), sem("xw_evac")
        s_rowst = [sem(f"xw_stored{h}") for h in range(2)]
        s_count = sem("tiles_counted")
        s_tab = sem("dve_table_step")
        s_start_st = sem("group_start_stored")
        s_idx = [sem(f"idx_in{h}") for h in range(2)]
        s_gath = [sem(f"gathered{h}") for h in range(2)]
        s_seen = sem("wait_over")
        s_ea = [sem(f"ea_in{h}") for h in range(2)]
        s_ew = [sem(f"ew_done{q}") for q in range(2)]
        s_msg = [sem(f"msg_done{h}") for h in range(2)]
        s_hotw = sem("hot_win_done")
        s_dist = sem("dist_done")
        s_win = [sem(f"win_mm{h}") for h in range(2)]
        s_add = [sem(f"yT_added{h}") for h in range(2)]
        s_rel = [sem(f"rel_key{h}") for h in range(2)]
        s_hot = [sem(f"hot_ready{h}") for h in range(2)]
        s_amm = [sem(f"a_mm{h}") for h in range(2)]
        s_aev = [sem(f"a_evac{j}") for j in range(GH)]
        s_ast = [sem(f"a_stored{h}") for h in range(2)]
        s_fin = {n: sem("l0_" + n) for n in ("mm", "add", "stats")}
        def sems(prefix, names):
            return {n: sem(prefix + n) for n in names.split()}

        s_norm = sems("norm_", "sqrt recip ready")
        s_walk = {1: sems("walk1_", "xn0 xn1 xs0 xs1 hi0 hi1 lo tp0 tp1 xnT lin yb0 yb1 y"),
                  2: sems("walk2_", "xn0 xn1 xs0 xs1 hi0 hi1 lo yb0 yb1"),
                  3: sems("walk3_", "xn0 xn1 xs0 xs1 hi0 hi1 lo tp0 tp1 xnT lin y st0 st1"),
                  4: sems("walk4_", "xn0 xn1 st0 st1")}
        S = sems("dense_", "at0 at1 main0 main1 evac0 evac1 lin0 lin1 y0 y1 stats0 stats1")
        s_deg = sems("deg_", "mm col red0 red1 sum0 sum1")
        s_gated = sems("gated_", "z0 z1 zt0 zt1 zts0 zts1 gate0 gate1 g0 g1 mix0 mix1")
        s_root = sem("roots")
        s_off = sem("fast_path_off_known")
        s_g = [sems("general0_", "in gathered0 place ew msg hot mm sum used done")] + 3 * [
            sems("general_", "table in gathered1 gathered2 gathered3 place msg hot mm sum used block lin done")]
        s_bn = sem("bn_dve")
        s_bn_pe = sem("bn_pe")
        s_bn_act = sem("bn_act")
        s_bn_pool = sem("bn_pool")
        s_x3 = sem("x3_back")

        block = ctx.enter_context(nc.Block())
        parts_v = [parts[:, k] for k in range(2)]
        at_v = [a.rearrange("p (c h d) -> p c h d", h=NB, d=SN) for a in at]
        BN_SRC = {1: x, 2: y, 3: y, 4: y}
        SRC_SCALE = {2: src_l2, 3: src_l3}
        WGT = {1: W_L1, 2: W_L2, 3: W_GCN}
        DST_SCALE = {1: scale_l1, 2: dst_l2, 3: dst_l3}

        def walk(eng, fn):
            with eng.Fori(0, NT // 2) as p:
                for s in range(2):
                    fn(2 * p + s, s, p)
            if NT % 2:
                fn(NT - 1, 0, NT // 2)

        def walk_ahead(eng, ahead, fn):
            assert NT % 2
            ahead(0, 0, 0)
            with eng.Fori(0, NT // 2) as p:
                ahead(2 * p + 1, 1, p)
                fn(2 * p, 0, p)
                ahead(2 * p + 2, 0, p + 1)
                fn(2 * p + 1, 1, p)
            fn(NT - 1, 0, NT // 2)

        def of(k, c, p):
            return (k - 1) * (NPAIR + 1 - c) + p

        def blocks(a, t):
            return a[:, bass.ds(t * BT, BT), :]

        def chunks(eng, fn):
            with eng.Fori(0, NPAIR) as p:
                fn(p, (0, 1), CB)
            fn(NPAIR, (0,), TAIL // P)

        big32 = BIG[:, :].bitcast(F32)
        sq = big32[:, 0:NP].rearrange("p (b f) -> p b f", f=D)
        x3b = big32[:, NP:2 * NP].rearrange("p (b f) -> p b f", f=D)
        xT = y[:, :, :].rearrange("p b f -> p (b f)")
        xwS = gath


        def off(eng):
            eng.wait_ge(s_off, 10)
            return eng.value_load(off_i[0:1, 0:1], min_val=0, max_val=1)

        def general_sync(sp, k, g_off):
            g = s_g[k]
            before = max(k - 1, 0)
            with sp.If(g_off > 0):
                if k == 0:
                    for h in range(2):
                        sp.wait_ge(s_gath[h], NI * 16 * T8)
                        sp.wait_ge(s_ew[h], 2 * NI + 1)
                    sp.wait_ge(s_ea[0], 16 * (NI + 1))
                else:
                    sp.wait_ge(s_walk[k]["lo"], NT)
                    for part_of in range(2):
                        sp.dma_start(rows_d[:, part_of * D:part_of * D + D].rearrange("(b p) f -> p b f", p=P), parts_v[part_of]).then_inc(g["table"], 16)
                with sp.Fori(0, NH) as n:
                    sp.wait_ge(g["used"], before * NH + n)
                    sp.dma_start(g_src[:, :], src_d[:, bass.ds(n * T8, T8)]).then_inc(g["in"], 16)
                    sp.dma_start(g_dst[:, :], dst_d[:, bass.ds(n * T8, T8)]).then_inc(g["in"], 16)
                    if k == 0:
                        sp.dma_start(ea[:, 0, :], ea_d[bass.ds(n, 1), :, :].rearrange("o p n -> (o p) n")).then_inc(g["in"], 16)
                sp.wait_ge(g["done"], before + 1)

        def general_pool(pool, k, g_off):
            g = s_g[k]
            before = max(k - 1, 0)
            with pool.If(g_off > 0):
                if k > 0:
                    pool.wait_ge(g["table"], 32 * (before + 1))
                with pool.Fori(0, NH) as n:
                    pool.wait_ge(g["in"], before * NH * loads(k) + n * loads(k) + loads(k))
                    pool.sem_inc(s_seen, 1)
                    for t in range(T8):
                        nc.gpsimd.indirect_dma_start(g_rows[k][:, t, :], None, rows_d if k > 0 else xw_d,
                                                     bass.IndirectOffsetOnAxis(ap=g_src[:, t:t + 1], axis=0)).then_inc(g[f"gathered{k}"], 16)

        def loads(k):
            return 48 if k == 0 else 32

        def general_pe(pe, k, g_off):
            g = s_g[k]
            before = max(k - 1, 0)
            with pe.If(g_off > 0):
                with pe.Fori(0, NH) as n:
                    if k == 0:
                        pe.wait_ge(g["in"], before * NH * loads(k) + n * loads(k) + loads(k))
                        for q in range(2):
                            last = nc.tensor.matmul(PB[:, q, :], ea[:, 0, :], edge_w[:, 4 * q:4 * q + 4, :], start=True, stop=True)
                        last.then_inc(g["ew"], 1)
                        pe.wait_ge(g["msg"], 2 * n + 2)
                    else:
                        pe.wait_ge(g[f"gathered{k}"], n * (16 * T8) + 16 * T8)
                    pe.sem_inc(s_seen, 1)
                    with pe.Fori(0, NB) as b:
                        pe.wait_ge(g["hot"], before * NH * NB + n * NB + b + 1)
                        pe.wait_ge(g["sum"], before * NH * NB + n * NB + b)
                        for t in range(T8):
                            ends = {"start": t == 0, "stop": t == T8 - 1}
                            if k == 0:
                                last = nc.tensor.matmul(PB[:, 2, 0:D], g_hot[0][:, t, :], msg[:, t, :], **ends)
                            else:
                                nc.tensor.matmul(PB[:, 2, 0:P], g_rows[k][:, t, 0:D], g_hot[k][:, t, :], start=(t == 0), stop=False)
                                last = nc.tensor.matmul(PB[:, 2, 0:P], g_rows[k][:, t, D:2 * D], g_hot[k][:, t, :], start=False, stop=(t == T8 - 1))
                        if k == 0:
                            for col, hot in ((0, g_hot_src), (1, g_hot[0])):
                                for t in range(T8):
                                    last = nc.tensor.matmul(PB[:, 3, col:col + 1], hot[:, t, :], ones[:, 0:1], start=(t == 0), stop=(t == T8 - 1))
                        last.then_inc(g["mm"], 1)
                if k > 0:
                    with pe.Fori(0, NB) as b:
                        pe.wait_ge(g["block"], before * NB + b + 1)
                        pe.wait_ge(g["lin"], before * NB + b)
                        nc.tensor.matmul(PB[:, 4, 0:D], g_block, wts[:, WGT[k], :], start=True, stop=True).then_inc(g["mm"], 1)
                pe.wait_ge(g["done"], before + 1)

        def general_dve(v, k, g_off):
            g = s_g[k]
            before = max(k - 1, 0)
            with v.If(g_off > 0):
                if k == 0:
                    v.wait_ge(s_hotw, 2 * NI + 1)
                    for h in range(2):
                        v.wait_ge(s_win[h], NI)
                else:
                    if k != 2:
                        v.wait_ge(s_walk[k]["y"], 2 * NT)
                    if k < 3:
                        for s in range(2):
                            v.wait_ge(s_walk[k][f"yb{s}"], TURNS[s])
                    nc.vector.memset(g_sum, 0.0)
                with v.Fori(0, NH) as n:
                    v.wait_ge(g["in"], before * NH * loads(k) + n * loads(k) + loads(k))
                    nc.vector.tensor_copy(g_place[:, 0, :], g_dst[:, :])
                    nc.vector.tensor_copy(g_place[:, 1, :], g_src[:, :]).then_inc(g["place"], 1)
                    v.wait_ge(g["place"], before * NH * (NB + 3) + n * (NB + 3) + 1)
                    nc.vector.tensor_scalar(g_pad[:, :], g_place[:, 0, :], float(N), float(4 * NP), ALU.is_ge, ALU.mult).then_inc(g["place"], 1)
                    v.wait_ge(g["place"], before * NH * (NB + 3) + n * (NB + 3) + 2)
                    nc.vector.tensor_tensor(g_place[:, 1, :], g_place[:, 1, :], g_pad[:, :], ALU.add).then_inc(g["place"], 1)
                    if k == 0:
                        v.wait_ge(g["ew"], n + 1)
                        v.wait_ge(g[f"gathered{k}"], n * (16 * T8) + 16 * T8)
                        for q in range(2):
                            nc.vector.tensor_tensor(msg[:, 4 * q:4 * q + 4, :], PB[:, q, :].rearrange("p (t f) -> p t f", f=D), g_rows[0][:, 4 * q:4 * q + 4, :], ALU.mult).then_inc(g["msg"], 1)
                    with v.Fori(0, NB) as b:
                        v.wait_ge(g["place"], before * NH * (NB + 3) + n * (NB + 3) + b + 3)
                        last = nc.vector.tensor_tensor(g_hot[k], cols_pf[:, :].unsqueeze(1).broadcast_to([P, T8, P]), g_place[:, 0, :].unsqueeze(2).broadcast_to([P, T8, P]), ALU.is_equal)
                        if k > 0:
                            last.then_inc(g["hot"], 1)
                        else:
                            nc.vector.tensor_tensor(g_hot_src, cols_pf[:, :].unsqueeze(1).broadcast_to([P, T8, P]), g_place[:, 1, :].unsqueeze(2).broadcast_to([P, T8, P]), ALU.is_equal).then_inc(g["hot"], 1)
                        v.wait_ge(g["mm"], before * (NH + 1) * NB + n * NB + b + 1)
                        nc.vector.tensor_scalar(g_place[:, :, :], g_place[:, :, :], float(-P), None, ALU.add).then_inc(g["place"], 1)
                        v.wait_ge(g["sum"], before * NH * NB + n * NB + b)
                        if k == 0:
                            nc.vector.tensor_tensor(x[:, bass.ds(b, 1), :], x[:, bass.ds(b, 1), :], PB[:, 2:3, 0:D], ALU.add)
                            nc.vector.tensor_tensor(g_deg[:, :, bass.ds(b, 1)], g_deg[:, :, bass.ds(b, 1)], PB[:, 3, 0:2].unsqueeze(2), ALU.add).then_inc(g["sum"], 1)
                        else:
                            nc.vector.tensor_tensor(g_sum[:, bass.ds(b * P, P)], g_sum[:, bass.ds(b * P, P)], PB[:, 2, 0:P], ALU.add).then_inc(g["sum"], 1)
                    v.wait_ge(g["sum"], before * NH * NB + n * NB + NB)
                    v.wait_ge(g["place"], before * NH * (NB + 3) + n * (NB + 3) + (NB + 3))
                    v.sem_inc(g["used"], 1)
                v.wait_ge(g["sum"], (before + 1) * NH * NB)
                if k > 0:
                    with v.Fori(0, NB) as b:
                        v.wait_ge(g["mm"], before * (NH + 1) * NB + NH * NB + b)
                        nc.vector.tensor_copy(g_block, g_sum[:, bass.ds(b * P, P)]).then_inc(g["block"], 1)
                        v.wait_ge(g["mm"], before * (NH + 1) * NB + NH * NB + b + 1)
                        nc.vector.scalar_tensor_tensor(out=y[:, bass.ds(b, 1), :].rearrange("p o f -> p (o f)"), in0=PB[:, 4, 0:D], scalar=DST_SCALE[k][:, bass.ds(b, 1)],
                                                       in1=y[:, bass.ds(b, 1), :].rearrange("p o f -> p (o f)"), op0=ALU.mult, op1=ALU.add).then_inc(g["lin"], 1)
                    v.wait_ge(g["lin"], (before + 1) * NB)
                v.sem_inc(g["done"], 1)

        @block.sync
        def _(sp):
            sp.dma_start(wts[:, :, :], w_d[0:7].rearrange("w k n -> k w n")).then_inc(s_in["w"], 16)
            with nc.allow_non_contiguous_dma(reason="128 numbers, once"):
                sp.dma_start(bias_l0[:, :], vec_d[0, B_L0, :].rearrange("(f o) -> f o", o=1)).then_inc(s_in["w"], 16)
            sp.dma_start(src_i, src_d).then_inc(s_in["edges"], 16)
            sp.dma_start(dst_i, dst_d).then_inc(s_in["edges"], 16)
            sp.dma_start(first_i, first_d.broadcast_to([P, T])).then_inc(s_in["firsts"], 16)
            sp.dma_start(half_i, half_d.broadcast_to([P, NH])).then_inc(s_in["firsts"], 16)
            for part_of, (c0, c1) in enumerate(((0, XT_CUT * BT * P), (XT_CUT * BT * P, NP))):
                sp.dma_start(xT[:, c0:c1], xT_d[:, c0:c1]).then_inc(s_in[f"xT{part_of}"], 16)
            sp.wait_ge(s_const, 1)
            for t in range(T8):
                sp.dma_start(edge_w[ED * t:ED * t + ED, t, :], w_d[7, 0:ED, :]).then_inc(s_in["edge_w"], 16)
            sp.dma_start(next_i, next_d).then_inc(s_in["rows"], 16)
            sp.dma_start(win_tab[:, :], half_d).then_inc(s_in["rows"], 16)
            for t in range(NT):
                sp.wait_ge(s_rowev, 2 * t + 2)
                sp.dma_start(xw_d[t * BT * P:(t + 1) * BT * P, :].rearrange("(b p) f -> p b f", p=P),
                             xwS[:, T8 * (t % 2):T8 * (t % 2) + BT, :]).then_inc(s_rowst[t % 2], 16)
            sp.dma_start(ea[:, 0, :], ea_d[0]).then_inc(s_ea[0], 16)
            with sp.Fori(0, NI) as i:
                for h in range(2):
                    sp.wait_ge(s_gath[h], i * (16 * T8))
                    sp.dma_start(idx[:, h, :], idx_d[bass.ds(2 * i + h, 1), :, :].rearrange("o p t -> (o p) t")).then_inc(s_idx[h], 16)
                    if h == 0:
                        sp.wait_ge(s_ew[1], 2 * i)
                        sp.dma_start(ea[:, 1, :], ea_d[bass.ds(2 * i + 1, 1), :, :].rearrange("o k e -> (o k) e")).then_inc(s_ea[1], 16)
                    else:
                        sp.wait_ge(s_ew[1], 2 * i + 1)
                        sp.dma_start(ea[:, 0, :], ea_d[bass.ds(2 * i + 2, 1), :, :].rearrange("o k e -> (o k) e")).then_inc(s_ea[0], 16)
            for h in range(2):
                sp.wait_ge(s_add[h], NI)
                sp.wait_ge(s_amm[h], NI * GH * GT)
                sp.wait_ge(s_ast[h], 16 * NI)
                sp.wait_ge(s_ew[h], NH + 1)
            sp.wait_ge(s_hotw, NH + 1)
            g_off = off(sp)
            general_sync(sp, 0, g_off)
            sp.wait_ge(s_deg["mm"], 1)
            for k in (1, 2, 3):
                general_sync(sp, k, g_off)

                def load(p, cs, nb):
                    for c in cs:
                        if k == 1:
                            sp.wait_ge(s_deg[f"sum{c}"], p * SB)
                        sp.wait_ge(S[f"main{c}"], of(k, c, p))
                        if k == 1:
                            sp.wait_ge(s_deg[f"red{c}"], p)
                        nh = nb * P // SN
                        sp.dma_start(at_d_of(c, nh), at_d[bass.ds(2 * CH * p + CH * c, nh), :, :].rearrange("h p n -> p h n")).then_inc(S[f"at{c}"], 16)

                def at_d_of(c, nh):
                    return at[c].rearrange("p (h n) -> p h n", h=CH)[:, 0:nh, :]

                if k == 2:
                    for c in range(2):
                        sp.wait_ge(s_deg[f"red{c}"], NPAIR + 1 - c)
                        sp.wait_ge(s_deg[f"sum{c}"], (NPAIR + 1 - c) * SB)
                chunks(sp, load)
            for c in range(2):
                sp.wait_ge(S[f"main{c}"], of(4, c, 0))
                sp.wait_ge(s_walk[3][f"st{c}"], 16 * TURNS[c])
            sp.dma_start(x3b, x3_d.rearrange("(b p) f -> p b f", p=P)).then_inc(s_x3, 16)
            Wk = s_walk[4]

            def store(t, s, p):
                sp.wait_ge(Wk[f"xn{s}"], p + 1)
                if p is NT // 2 and s == 0:
                    sp.dma_start(out_d[t * BT * P:(NB - 1) * P, :].rearrange("(b p) f -> p b f", p=P), xn[s][:, 0:BT - 1, :]).then_inc(Wk[f"st{s}"], 16)
                    sp.dma_start(out_d[(NB - 1) * P:N, :], xn[s][0:LAST, BT - 1, :]).then_inc(Wk[f"st{s}"], 16)
                else:
                    sp.dma_start(out_d[bass.ds(t * (BT * P), BT * P), :].rearrange("(b p) f -> p b f", p=P), xn[s]).then_inc(Wk[f"st{s}"], 16)

            walk(sp, store)
            sp.wait_ge(Wk["st0"], 16 * (NT // 2 + 2 * (NT % 2)))
            sp.wait_ge(Wk["st1"], 16 * TURNS[1])

        @block.gpsimd
        def _(pool):
            nc.gpsimd.memset(edge_w[:, :, :], 0.0).then_inc(s_const, 1)
            nc.gpsimd.memset(ident[:, :], 0.0)
            nc.gpsimd.memset(x[:, NB - 1, :], 0.0).then_inc(s_const, 1)
            pool.wait_ge(s_const, 2)
            nc.gpsimd.affine_select(out=ident[:, :], in_=ident[:, :], compare_op=ALU.not_equal, fill=1.0,
                                    base=0, pattern=[[-1, P]], channel_multiplier=1)
            nc.gpsimd.memset(ones[:, :], 1.0)
            nc.gpsimd.memset(ones16[:, :], 1.0)
            nc.gpsimd.iota(cols_key[:, :], [[1, NB], [NB, GN]], base=0, channel_multiplier=0, allow_small_or_imprecise_dtypes=True)
            nc.gpsimd.iota(cols_p[:, :], [[1, P]], base=0, channel_multiplier=0, allow_small_or_imprecise_dtypes=True)
            nc.gpsimd.iota(cols_pf[:, :], [[1, P]], base=0, channel_multiplier=0, allow_small_or_imprecise_dtypes=True)
            nc.gpsimd.iota(group_dst[:, :], [[P * GN, GC]], base=0, channel_multiplier=GN, allow_small_or_imprecise_dtypes=True)
            nc.gpsimd.memset(eps_ln[:, 0:1], 1.0)
            nc.gpsimd.memset(flags[:, :], 0.0)
            nc.gpsimd.memset(stage[:, :, :], 0.0)
            nc.gpsimd.memset(g_deg, 0.0)
            nc.gpsimd.memset(eps_ln[:, 1:2], 1e-5)
            nc.gpsimd.memset(eps_ln[:, 2:3], 1e-6)
            nc.gpsimd.memset(eps_ln[:, 3:4], 0.0)
            nc.gpsimd.iota(valid[:, :], [[0, 1]], base=0, channel_multiplier=1, allow_small_or_imprecise_dtypes=True)
            nc.gpsimd.iota(neg_group_key[:, :], [[-W, G]], base=0, channel_multiplier=0, allow_small_or_imprecise_dtypes=True).then_inc(s_const, 1)
            pool.wait_ge(s_in["w"], 32)
            nc.gpsimd.tensor_copy(yT[:, :], bias_l0[:, 0:1].broadcast_to([P, YW])).then_inc(s_const, 1)
            for h in range(2):
                pool.wait_ge(s_rowst[h], 16 * TURNS[h])
            with pool.Fori(0, NI) as i:
                for h in range(2):
                    pool.wait_ge(s_msg[h], i * 2)
                    pool.wait_ge(s_idx[h], i * 16 + 16)
                    pool.sem_inc(s_seen, 1)
                    for t in range(T8):
                        nc.gpsimd.indirect_dma_start(gath[:, T8 * h + t, :], None, xw_d,
                                                     bass.IndirectOffsetOnAxis(ap=idx[:, h, t:t + 1], axis=0)).then_inc(s_gath[h], 16)
            g_off = off(pool)
            general_pool(pool, 0, g_off)
            for k, bias in ((1, B_L1), (2, B_L2), (3, None)):
                Wk = s_walk[k]
                if k == 1:
                    for h in range(2):
                        pool.wait_ge(s_amm[h], NI * GH * GT)

                def residual(t, s, p):
                    pool.wait_ge(Wk[f"xn{s}"], p + 1)
                    if k < 3:
                        nc.gpsimd.tensor_tensor(blocks(y, t), xn[s], vecs[:, bias, :].unsqueeze(1).broadcast_to([P, BT, D]), ALU.add).then_inc(Wk[f"yb{s}"], 1)
                    else:
                        pool.dma_start(x3_d[bass.ds(t * (BT * P), BT * P), :].rearrange("(b p) f -> p b f", p=P), xn[s]).then_inc(Wk[f"st{s}"], 16)

                walk(pool, residual)
                general_pool(pool, k, g_off)
            pool.wait_ge(s_x3, 16)
            nc.gpsimd.tensor_tensor(x3b, x3b, vecs[:, BN_BETA, :].unsqueeze(1).broadcast_to([P, NB, D]), ALU.add).then_inc(s_bn_pool, 1)

        @block.vector
        def _(v):
            v.wait_ge(s_in["edges"], 32)
            v.wait_ge(s_in["firsts"], 32)
            v.wait_ge(s_const, 3)
            nc.vector.memset(rel[:, T:T + T8], 0.0)
            nc.vector.memset(key[:, T:TT], -1.0)
            nc.vector.memset(src_lo[:, T:TT], -1.0)
            nc.vector.tensor_scalar(src_hi_i, src_i, 7, None, ALU.logical_shift_right).then_inc(s_tab, 1)
            nc.vector.tensor_scalar(less.bitcast(I32), src_i, P - 1, None, ALU.bitwise_and).then_inc(s_tab, 1)
            nc.vector.tensor_copy(first_f, first_i).then_inc(s_tab, 1)
            v.wait_ge(s_tab, 2)
            nc.vector.scalar_tensor_tensor(out=key[:, 0:T], in0=dst_i, scalar=float(NB), in1=src_hi_i, op0=ALU.mult, op1=ALU.add).then_inc(s_tab, 1)
            nc.vector.tensor_copy(src_lo[:, 0:T], less.bitcast(I32)).then_inc(s_tab, 1)
            nc.vector.tensor_tensor(rel[:, 0:T].rearrange("p (n t) -> p n t", t=T8), half_i.unsqueeze(2).broadcast_to([P, NH, T8]),
                                    dst_i.rearrange("p (n t) -> p n t", t=T8), ALU.subtract).then_inc(s_tab, 1)
            v.wait_ge(s_tab, 6)
            for c in range(GC):
                last = nc.vector.tensor_scalar(less, first_f, group_dst[:, c:c + 1], None, ALU.is_lt, ALU.add, accum_out=start_f[:, c:c + 1])
                if c < GC - 1:
                    last = last.then_inc(s_count, 1)
                    v.wait_ge(s_count, c + 1)
            last.then_inc(s_tab, 1)
            v.wait_ge(s_tab, 7)
            nc.vector.tensor_scalar(start_i[:, :], start_f[:, :], -1.0, 0.0, ALU.add, ALU.max).then_inc(s_tab, 1)
            v.wait_ge(s_tab, 8)
            nc.vector.scalar_tensor_tensor(out=less, in0=dst_i, scalar=float(N), in1=rel[:, 0:T], op0=ALU.is_lt, op1=ALU.mult).then_inc(s_off, 1)
            v.wait_ge(s_off, 1)
            nc.vector.tensor_scalar(less, less, float(1 - WIN), None, ALU.is_lt, ALU.add, accum_out=flags[:, 0:1]).then_inc(s_off, 1)
            v.wait_ge(s_in["rows"], 32)
            v.wait_ge(s_off, 2)
            nc.vector.tensor_tensor(less, next_i, dst_i, ALU.is_lt).then_inc(s_off, 1)
            v.wait_ge(s_off, 3)
            nc.vector.tensor_scalar(less, less, 0.0, None, ALU.is_gt, ALU.add, accum_out=flags[:, 1:2]).then_inc(s_off, 1)
            v.wait_ge(s_in["start"], 16)
            v.wait_ge(s_off, 4)
            ng = NP // GN
            nc.vector.tensor_tensor(less[0:1, 0:ng], start_tab[0:1, 1:ng + 1], start_tab[0:1, 0:ng], ALU.subtract).then_inc(s_off, 1)
            v.wait_ge(s_off, 5)
            nc.vector.tensor_scalar(less[0:1, 0:ng], less[0:1, 0:ng], float(GT - 1), None, ALU.is_gt, ALU.add, accum_out=flags[0:1, 2:3]).then_inc(s_off, 1)
            v.wait_ge(s_off, 7)
            nc.vector.tensor_reduce(out=off_f[:, :], in_=PB[:, 7, 0:3], axis=AX.X, op=ALU.add).then_inc(s_off, 1)
            v.wait_ge(s_off, 8)
            nc.vector.tensor_scalar(off_f[:, :], off_f[:, :], 1.0, None, ALU.min).then_inc(s_off, 1)
            v.wait_ge(s_off, 9)
            nc.vector.tensor_copy(off_i[:, :], off_f[:, :])
            nc.vector.scalar_tensor_tensor(out=win_cols[:, :], in0=off_f[:, :].broadcast_to([P, WIN]), scalar=float(4 * NP), in1=cols_pf[:, 0:WIN], op0=ALU.mult, op1=ALU.add)
            nc.vector.scalar_tensor_tensor(out=cols_p[:, :], in0=off_f[:, :].broadcast_to([P, P]), scalar=float(4 * P), in1=cols_pf[:, :], op0=ALU.mult, op1=ALU.add).then_inc(s_off, 1)
            v.wait_ge(s_off, 10)
            v.wait_ge(s_rowxw, 2 * NT)
            v.wait_ge(s_const, 4)
            with v.Fori(0, NI) as i:
                for h in range(2):
                    n = 2 * i + h
                    win_at = v.value_load(win_tab[0:1, bass.ds(i * 2 + h, 1)], min_val=0, max_val=NP)
                    _, first_tile = nc.values_load_multi_w_load_instructions(start_tab[0:1, bass.ds(i * (2 * GH) + GH * h, GH)],
                                                                             engines=DVE_ONLY, min_val=0, max_val=T - 1, skip_runtime_bounds_check_because="a count of tiles, less one")
                    v.wait_ge(s_win[h], i)
                    for q in range(2):
                        v.wait_ge(s_ew[q], n + 1)
                        if q == 0:
                            v.wait_ge(s_gath[h], i * (16 * T8) + 16 * T8)
                        b = T8 * h + 4 * q
                        nc.vector.tensor_tensor(msg[:, b:b + 4, :], PB[:, q, :].rearrange("p (t f) -> p t f", f=D), gath[:, b:b + 4, :], ALU.mult).then_inc(s_msg[h], 1)
                    for j in range(GH):
                        v.wait_ge(s_rel[h], i * GH + (j + 1))
                        for k in range(GT):
                            s = GT * j + k
                            if s == 0:
                                v.wait_ge(s_amm[h], i * (GH * GT))
                            nc.vector.tensor_scalar(hot_lo[:, GH * GT * h + s, :], cols_p[:, :], src_lo[:, bass.ds(first_tile[j] + k, 1)], None, ALU.is_equal)
                            nc.vector.tensor_scalar(hot_key[:, GH * GT * h + s, :], cols_key[:, :], rel_key[:, GH * h + j, k:k + 1], None, ALU.is_equal).then_inc(s_hot[h], 1)
                    v.wait_ge(s_win[h], i + 1)
                    v.wait_ge(s_add[1 - h], i + h)
                    where = yT[:, bass.ds(win_at, WIN)]
                    nc.vector.tensor_tensor(where, where, PB[:, 2 + h, 0:WIN], ALU.add)
                    nc.vector.tensor_reduce(out=deg_row[0:1, bass.ds(i * (2 * SN) + h * SN, SN)], in_=PB[0:1, 2 + h, WIN:WIN + BT * SN].rearrange("p (b d) -> p d b", d=SN),
                                            axis=AX.X, op=ALU.add).then_inc(s_add[h], 1)

            F = s_fin

            def finish(t, s, p):
                v.wait_ge(F["mm"], t + 1)
                for q, nb in ((0, 4), (1, BT - 4)):
                    here = x[:, bass.ds(t * BT + 4 * q, nb), :]
                    nc.vector.tensor_tensor(here, here, PB[:, 2 * s + q, 0:nb * P].rearrange("p (b f) -> p b f", f=D), ALU.add).then_inc(F["add"], 1)
                v.wait_ge(F["add"], 2 * t + 2)
                v.sem_inc(s_seen, 1)
                for b in range(BT):
                    last = nc.vector.bn_stats(stats[:, 0, b, :], x[:, bass.ds(t * BT + b, 1), :].rearrange("p o f -> p (o f)"))
                last.then_inc(F["stats"], 1)
                v.wait_ge(F["stats"], 3 * t + 1)
                v.sem_inc(s_seen, 1)
                for b in range(BT):
                    last = nc.vector.bn_aggr(mv_turn[:, 0, b, :], stats[:, 0, b, :])
                last.then_inc(F["stats"], 1)
                v.wait_ge(F["stats"], 3 * t + 2)
                nc.vector.tensor_copy(mean_var[:, bass.ds(t * BT, BT), :], mv_turn[:, 0, :, :]).then_inc(F["stats"], 1)

            v.wait_ge(s_in["x"], 32)
            g_off = off(v)
            general_dve(v, 0, g_off)
            walk(v, finish)

            def norm(k):
                v.wait_ge(s_norm["sqrt"], k)
                nc.vector.reciprocal(rstd[:, :], rstd[:, :]).then_inc(s_norm["recip"], 1)
                v.wait_ge(s_norm["recip"], k)
                nc.vector.scalar_tensor_tensor(out=shift[:, :], in0=mean_var[:, :, 0], scalar=-1.0, in1=rstd[:, :], op0=ALU.mult, op1=ALU.mult).then_inc(s_norm["ready"], 1)

            for k in (1, 2, 3):
                norm(k)
                Wk = s_walk[k]

                def scaled(t, s, p):
                    v.wait_ge(Wk[f"xn{s}"], p + 1)
                    v.wait_ge(Wk[f"hi{s}"], p)
                    if not (isinstance(t, int) and t == 0):
                        v.wait_ge(Wk["lo"], t - 1)
                    if k == 1:
                        nc.vector.tensor_scalar(xs[s], xn[s], SCALE, None, ALU.mult).then_inc(Wk[f"xs{s}"], 1)
                    else:
                        nc.vector.tensor_tensor(xs[s], xn[s], SRC_SCALE[k][:, bass.ds(t * BT, BT)].unsqueeze(2).broadcast_to([P, BT, D]), ALU.mult).then_inc(Wk[f"xs{s}"], 1)

                def split(t, s, p):
                    if k != 2:
                        v.wait_ge(Wk["lin"], t)
                        v.wait_ge(Wk[f"tp{s}"], p + 1)
                        for q, nb in ((0, 4), (1, BT - 4)):
                            last = nc.vector.tensor_copy(xnT[:, 4 * q:4 * q + nb, :], PB[:, 2 - 2 * s + q, 0:nb * P].rearrange("p (b f) -> p b f", f=D))
                        last.then_inc(Wk["xnT"], 1)
                    v.wait_ge(Wk[f"hi{s}"], p + 1)
                    nc.vector.tensor_tensor(blocks(parts_v[1], t), xs[s], blocks(parts_v[0], t), ALU.subtract).then_inc(Wk["lo"], 1)
                    if k == 1:
                        v.wait_ge(Wk["lin"], t + 1)
                        v.wait_ge(Wk[f"yb{s}"], p + 1)
                        for q, nb in ((0, 4), (1, BT - 4)):
                            here = y[:, bass.ds(t * BT + 4 * q, nb), :]
                            nc.vector.tensor_tensor(here, here, PB[:, 4 + q, 0:nb * P].rearrange("p (b f) -> p b f", f=D), ALU.add).then_inc(Wk["y"], 1)
                    if k == 3:
                        v.wait_ge(Wk["lin"], t + 1)
                        for q, nb in ((0, 4), (1, BT - 4)):
                            nc.vector.tensor_tensor(x[:, bass.ds(t * BT + 4 * q, nb), :], PB[:, 4 + q, 0:nb * P].rearrange("p (b f) -> p b f", f=D),
                                                    vecs[:, B_LIN, :].unsqueeze(1).broadcast_to([P, nb, D]), ALU.add)
                            for b in range(4 * q, 4 * q + nb):
                                last = nc.vector.scalar_tensor_tensor(out=y[:, bass.ds(t * BT + b, 1), :].rearrange("p o f -> p (o f)"), in0=PB[:, 6 + q, (b - 4 * q) * P:(b - 4 * q + 1) * P],
                                                                      scalar=self_l3[:, bass.ds(t * BT + b, 1)], in1=vecs[:, B_GCN, :], op0=ALU.mult, op1=ALU.add)
                            last.then_inc(Wk["y"], 1)

                walk_ahead(v, scaled, split)
                if k == 1:
                    v.wait_ge(s_deg["mm"], 1)
                    nc.vector.tensor_tensor(deg, PB[:, 7, 0:NB], g_deg[:, 1, :], ALU.add).then_inc(s_deg["col"], 1)
                    v.wait_ge(s_deg["col"], 1)
                    nc.vector.tensor_scalar(scale_l1, deg, 1.0, SCALE, ALU.max, ALU.mult).then_inc(s_deg["col"], 1)
                    v.wait_ge(s_deg["col"], 2)
                    nc.vector.reciprocal(scale_l1, scale_l1).then_inc(s_deg["col"], 1)
                    v.wait_ge(s_deg["col"], 3)
                general_dve(v, k, g_off)

                def dense(p, cs, nb):
                    at_block = [CB * (2 * p + c) for c in range(2)]
                    if k == 1:
                        for c in cs:
                            v.wait_ge(S[f"at{c}"], 16 * of(k, c, p + 1))
                            nc.vector.tensor_reduce(out=sdeg_part[:, bass.ds(2 * p + c, 1), SB:NB].rearrange("p o b -> p (o b)"),
                                                    in_=at_v[c][:, 0:nb * P // SN, SB:NB, :].rearrange("p c h d -> p h c d"), axis=AX.XY, op=ALU.add).then_inc(s_deg[f"red{c}"], 1)
                    for c in cs:
                        v.wait_ge(S[f"lin{c}"], of(k, c, p + 1))
                        if k == 3:
                            v.wait_ge(s_gated[f"zt{c}"], p)
                            v.wait_ge(s_gated[f"mix{c}"], 5 * p)
                        for b in range(nb):
                            row = y[:, bass.ds(at_block[c] + b, 1), :].rearrange("p o f -> p (o f)")
                            last = nc.vector.scalar_tensor_tensor(out=zpre[c][:, b * P:b * P + P] if k == 3 else row, in0=PB[:, 4 + c, b * P:b * P + P],
                                                                  scalar=DST_SCALE[k][:, bass.ds(at_block[c] + b, 1)], in1=row, op0=ALU.mult, op1=ALU.add)
                        last.then_inc(S[f"y{c}"], 1)
                    if k == 3:
                        for c in cs:
                            n = nb * P
                            v.wait_ge(s_gated[f"gate{c}"], p + 1)
                            nc.vector.tensor_tensor(gate[c][:, 0:n].rearrange("p (b f) -> p b f", f=D), PB[:, 6 + c, 0:n].rearrange("p (b f) -> p b f", f=D),
                                                    vecs[:, B_GATE, :].unsqueeze(1).broadcast_to([P, nb, D]), ALU.add).then_inc(s_gated[f"mix{c}"], 1)
                    for c in cs:
                        if k < 3:
                            v.wait_ge(S[f"y{c}"], of(k, c, p + 1))
                            v.sem_inc(s_seen, 1)
                            for b in range(nb):
                                last = nc.vector.bn_stats(stats[:, c, b, :], y[:, bass.ds(at_block[c] + b, 1), :].rearrange("p o f -> p (o f)"))
                            last.then_inc(S[f"stats{c}"], 1)
                            v.wait_ge(S[f"stats{c}"], 3 * of(k, c, p) + 1)
                            v.sem_inc(s_seen, 1)
                            for b in range(nb):
                                last = nc.vector.bn_aggr(mv_turn[:, c, b, :], stats[:, c, b, :])
                            last.then_inc(S[f"stats{c}"], 1)
                            v.wait_ge(S[f"stats{c}"], 3 * of(k, c, p) + 2)
                            nc.vector.tensor_copy(mean_var[:, bass.ds(at_block[c], nb), :], mv_turn[:, c, 0:nb, :]).then_inc(S[f"stats{c}"], 1)
                        else:
                            n = nb * P
                            xl = x[:, bass.ds(at_block[c], nb), :].rearrange("p b f -> p (b f)")
                            v.wait_ge(s_gated[f"z{c}"], p + 1)
                            v.wait_ge(s_gated[f"zt{c}"], p + 1)
                            nc.vector.tensor_tensor(zpre[c][:, 0:n], zpre[c][:, 0:n], xl, ALU.subtract).then_inc(s_gated[f"mix{c}"], 1)
                            v.wait_ge(s_gated[f"mix{c}"], 5 * p + 2)
                            v.wait_ge(s_gated[f"g{c}"], p + 1)
                            nc.vector.tensor_tensor(zpre[c][:, 0:n], zpre[c][:, 0:n], gate[c][:, 0:n], ALU.mult).then_inc(s_gated[f"mix{c}"], 1)
                            v.wait_ge(s_gated[f"mix{c}"], 5 * p + 3)
                            nc.vector.tensor_tensor(zpre[c][:, 0:n], zpre[c][:, 0:n], xl, ALU.add).then_inc(s_gated[f"mix{c}"], 1)
                            v.wait_ge(s_gated[f"mix{c}"], 5 * p + 4)
                            nc.vector.tensor_scalar(xl, zpre[c][:, 0:n], 0.0, None, ALU.max).then_inc(s_gated[f"mix{c}"], 1)

                chunks(v, dense)
                if k == 1:
                    for c in range(2):
                        v.wait_ge(s_deg[f"red{c}"], NPAIR + 1 - c)
                        v.wait_ge(s_deg[f"sum{c}"], (NPAIR + 1 - c) * SB)
                    nc.vector.tensor_reduce(out=sdeg, in_=sdeg_part[:, 0:NCH + 1, :].rearrange("p c b -> p b c"), axis=AX.X, op=ALU.add).then_inc(s_root, 1)
                    v.wait_ge(s_root, 1)
                    nc.vector.tensor_scalar(roots[:, 0, :], sdeg, 1.0, 1e-6, ALU.max, ALU.add).then_inc(s_root, 1)
                    nc.vector.tensor_scalar(roots[:, 1, :], deg, 1e-6, None, ALU.add).then_inc(s_root, 1)
                    nc.vector.tensor_scalar(roots[:, 2, :], deg, 1.0, 1e-12, ALU.add, ALU.max).then_inc(s_root, 1)
                    v.wait_ge(s_root, 5)
                    nc.vector.reciprocal(roots, roots).then_inc(s_root, 1)
                    v.wait_ge(s_root, 6)
                    nc.vector.tensor_scalar(src_l2, roots[:, 0, :], SCALE, None, ALU.mult).then_inc(s_root, 1)
                    nc.vector.tensor_scalar(dst_l2, roots[:, 1, :], 1 / SCALE, None, ALU.mult).then_inc(s_root, 1)
                    nc.vector.tensor_scalar(src_l3, roots[:, 2, :], SCALE, None, ALU.mult).then_inc(s_root, 1)
                    nc.vector.tensor_scalar(dst_l3, roots[:, 2, :], 1 / SCALE, None, ALU.mult).then_inc(s_root, 1)
                    nc.vector.tensor_tensor(self_l3, roots[:, 2, :], roots[:, 2, :], ALU.mult).then_inc(s_root, 1)
                    v.wait_ge(s_root, 11)

            step = [0]

            def bn(instruction):
                instruction.then_inc(s_bn, 1)
                step[0] += 1

            for c in range(2):
                v.wait_ge(s_gated[f"mix{c}"], 5 * (NPAIR + 1 - c))
            bn(nc.vector.tensor_scalar(valid[:, :], valid[:, :], float(LAST), None, ALU.is_lt))
            v.wait_ge(s_bn, 1)
            bn(nc.vector.tensor_scalar(x[:, NB - 1, :], x[:, NB - 1, :], valid[:, :], None, ALU.mult))
            v.wait_ge(s_bn, 2)
            bn(nc.vector.tensor_reduce(out=bn_row[:, 0, :], in_=x[:, :, :].rearrange("p b f -> p f b"), axis=AX.X, op=ALU.add))
            v.wait_ge(s_bn_pe, 1)
            bn(nc.vector.tensor_scalar(bn_row[:, 1, :], PB[:, 0, 0:D], 1.0 / N, None, ALU.mult))
            v.wait_ge(s_bn, 4)
            bn(nc.vector.tensor_tensor(y[:, :, :], x[:, :, :], bn_row[:, 1, :].unsqueeze(1).broadcast_to([P, NB, D]), ALU.subtract))
            v.wait_ge(s_bn, 5)
            bn(nc.vector.tensor_scalar(y[:, NB - 1, :], y[:, NB - 1, :], valid[:, :], None, ALU.mult))
            v.wait_ge(s_bn_act, 1)
            bn(nc.vector.tensor_reduce(out=bn_row[:, 2, :], in_=sq.rearrange("p b f -> p f b"), axis=AX.X, op=ALU.add))
            v.wait_ge(s_bn_act, 2)
            bn(nc.vector.reciprocal(bn_row[:, 3, :], bn_row[:, 3, :]))
            v.wait_ge(s_bn, 8)
            bn(nc.vector.tensor_tensor(bn_row[:, 3, :], bn_row[:, 3, :], vecs[:, BN_GAMMA, :], ALU.mult))
            v.wait_ge(s_bn, 9)
            bn(nc.vector.tensor_tensor(y[:, :, :], y[:, :, :], bn_row[:, 3, :].unsqueeze(1).broadcast_to([P, NB, D]), ALU.mult))
            v.wait_ge(s_bn, 10)
            v.wait_ge(s_bn_pool, 1)
            bn(nc.vector.tensor_tensor(y[:, :, :], y[:, :, :], x3b, ALU.add))
            v.wait_ge(s_bn, 11)
            for b0 in range(0, NB, BT):
                for b in range(BT):
                    last = nc.vector.bn_stats(stats[:, b0 // BT % 2, b, :], y[:, b0 + b, :])
                bn(last)
                v.wait_ge(s_bn, step[0])
                for b in range(BT):
                    last = nc.vector.bn_aggr(mean_var[:, b0 + b, :], stats[:, b0 // BT % 2, b, :])
            bn(last)
            norm(4)

        @block.tensor
        def _(pe):
            pe.wait_ge(s_in["w"], 32)
            for t in range(NT):
                if t in (0, XT_CUT):
                    pe.wait_ge(s_in[f"xT{int(t > 0)}"], 16)
                for b in range(BT):
                    if b % 4 == 0 and t >= 2:
                        pe.wait_ge(s_rowev, 2 * (t - 2) + b // 4 + 1)
                    last = nc.tensor.matmul(PB[:, 2 * (t % 2) + b // 4, b % 4 * P:b % 4 * P + P], xT[:, (t * BT + b) * P:(t * BT + b + 1) * P], wts[:, W_L0, :], start=True, stop=True)
                    if b in (3, BT - 1):
                        last.then_inc(s_rowxw, 1)
            pe.wait_ge(s_in["edge_w"], 16 * T8)

            def edge_products(h, n):
                for q in range(2):
                    nc.tensor.matmul(PB[:, q, :], ea[:, h, :], edge_w[:, 4 * q:4 * q + 4, :], start=True, stop=True).then_inc(s_ew[q], 1)

            def degree_products(h):
                for q in range(NT):
                    nc.tensor.matmul(PB[0:1, 2 + h, WIN:WIN + BT * SN], ones16[:, 0:1], stage[:, h, q * BT * SN:(q + 1) * BT * SN],
                                     start=(q == 0), stop=(q == NT - 1))

            pe.wait_ge(s_rowev, 2 * NT)
            pe.wait_ge(s_ea[0], 16)
            pe.wait_ge(s_const, 3)
            edge_products(0, 0)
            degree_products(0)
            pe.wait_ge(s_off, 6)
            nc.tensor.matmul(PB[:, 7, 0:3], ones[:, :], flags[:, :], start=True, stop=True).then_inc(s_off, 1)
            with pe.Fori(0, NI) as i:
                for h in range(2):
                    n = 2 * i + h
                    for j in range(GH):
                        if j == 0:
                            pe.wait_ge(s_msg[h], i * 2 + 2)
                            pe.wait_ge(s_hotw, n + 1)
                            for t in range(T8):
                                last = nc.tensor.matmul(PB[:, 2 + h, 0:WIN], msg[:, T8 * h + t, :], hot_win[:, T8 * h + t, :], start=(t == 0), stop=(t == T8 - 1))
                            last.then_inc(s_win[h], 1)
                            pe.wait_ge(s_ea[1 - h], i * 16 + 16 * (1 + h))
                            edge_products(1 - h, n + 1)
                        pe.wait_ge(s_aev[j], n)
                        for k in range(GT):
                            s = GT * j + k
                            pe.wait_ge(s_hot[h], i * (GH * GT) + (s + 1))
                            nc.tensor.matmul(PB[:, 4 + j, 0:W], hot_lo[:, GH * GT * h + s, :], hot_key[:, GH * GT * h + s, :],
                                             start=(k == 0), stop=(k == GT - 1)).then_inc(s_amm[h], 1)
                    pe.wait_ge(s_add[1 - h], i + h)
                    degree_products(1 - h)

            for h in range(2):
                pe.wait_ge(s_add[h], NI)
            g_off = off(pe)
            general_pe(pe, 0, g_off)
            pe.wait_ge(s_aev[GH - 1], NH)
            for t in range(NT):
                if t >= 2:
                    pe.wait_ge(s_fin["add"], 2 * t - 2)
                for b in range(BT):
                    last = nc.tensor.transpose(PB[:, 2 * (t % 2) + b // 4, b % 4 * P:b % 4 * P + P], yT[:, (t * BT + b) * P:(t * BT + b + 1) * P], ident[:, :])
                last.then_inc(s_fin["mm"], 1)
                for b in range(t * BT, t * BT + BT):
                    last = nc.tensor.matmul(PB[:, 7, b:b + 1], deg_row[0:1, 2 * SN + b * P:2 * SN + b * P + P], ones[0:1, 0:1], start=True, stop=True)
            last.then_inc(s_deg["mm"], 1)
            for k in (1, 2, 3):
                Wk = s_walk[k]

                def turned(t, s, p):
                    pe.wait_ge(Wk[f"xn{s}"], p + 1)
                    if not (isinstance(t, int) and t == 0):
                        pe.wait_ge(Wk["xnT"], t - 1)
                    for b in range(BT):
                        last = nc.tensor.transpose(PB[:, 2 - 2 * s + b // 4, b % 4 * P:b % 4 * P + P], xn[s][:, b, :], ident[:, :])
                    last.then_inc(Wk[f"tp{s}"], 1)

                def linear(t, s, p):
                    pe.wait_ge(Wk["xnT"], t + 1)
                    pe.wait_ge(Wk["y"], 2 * t)
                    for b in range(BT):
                        for bank, w in ((4, W_R1),) if k == 1 else ((4, W_LIN), (6, W_GCN)):
                            last = nc.tensor.matmul(PB[:, bank + b // 4, b % 4 * P:b % 4 * P + P], xnT[:, b, :], wts[:, w, :], start=True, stop=True)
                    last.then_inc(Wk["lin"], 1)

                if k != 2:
                    walk_ahead(pe, turned, linear)
                    pe.wait_ge(Wk["lo"], NT)
                    pe.wait_ge(Wk["y"], 2 * NT)
                general_pe(pe, k, g_off)

                def dense(p, cs, nb, late=None):
                    n = nb * P
                    for c in cs:
                        pe.wait_ge(S[f"at{c}"], 16 * of(k, c, p + 1))
                        pe.wait_ge(S[f"evac{c}"], of(k, c, p))
                        if late and c == 0 and len(cs) == 1:
                            turned_z(*late)
                        for b in range(NB):
                            if late and c == len(cs) - 1 and b == NB // 4:
                                gate_products(*late)
                            if k == 2 and c == 0 and b % BT == 0:
                                pe.wait_ge(Wk["lo"], b // BT + 1)
                            piece = at_v[c][:, 0:n // SN, b, :]
                            nc.tensor.matmul(PB[:, c, 0:n], parts_v[0][:, b, :], piece, start=(b == 0), stop=False)
                            last = nc.tensor.matmul(PB[:, c, 0:n], parts_v[1][:, b, :], piece, start=False, stop=(b == NB - 1))
                        last.then_inc(S[f"main{c}"], 1)
                        if late and c == 0 and len(cs) == 2:
                            turned_z(*late)
                    for c in cs:
                        pe.wait_ge(S[f"evac{c}"], of(k, c, p + 1))
                        pe.wait_ge(S[f"y{c}"], of(k, c, p))
                        for b in range(nb):
                            last = nc.tensor.matmul(PB[:, 4 + c, b * P:b * P + P], aggT[c][:, b * P:b * P + P], wts[:, WGT[k], :], start=True, stop=True)
                        last.then_inc(S[f"lin{c}"], 1)

                def turned_z(p, cs, nb):
                    for c in cs:
                        pe.wait_ge(s_gated[f"z{c}"], p + 1)
                        pe.wait_ge(s_gated[f"zts{c}"], p)
                        for b in range(nb):
                            last = nc.tensor.transpose(PB[:, 2 + c, b * P:b * P + P], zpre[c][:, b * P:b * P + P], ident[:, :])
                        last.then_inc(s_gated[f"zt{c}"], 1)

                def gate_products(p, cs, nb):
                    for c in cs:
                        pe.wait_ge(s_gated[f"g{c}"], p)
                        pe.wait_ge(s_gated[f"zts{c}"], p + 1)
                        for b in range(nb):
                            last = nc.tensor.matmul(PB[:, 6 + c, b * P:b * P + P], zT[c][:, b * P:b * P + P], wts[:, W_GATE, :], start=True, stop=True)
                        last.then_inc(s_gated[f"gate{c}"], 1)

                if k < 3:
                    chunks(pe, dense)
                else:
                    dense(0, (0, 1), CB, late=None)
                    with pe.Fori(1, NPAIR) as p:
                        dense(p, (0, 1), CB, late=(p - 1, (0, 1), CB))
                    dense(NPAIR, (0,), TAIL // P, late=(NPAIR - 1, (0, 1), CB))
                    turned_z(NPAIR, (0,), TAIL // P)
                    gate_products(NPAIR, (0,), TAIL // P)
            pe.wait_ge(s_bn, 3)
            nc.tensor.matmul(PB[:, 0, 0:D], ones[:, :], bn_row[:, 0, :], start=True, stop=True).then_inc(s_bn_pe, 1)
            pe.wait_ge(s_bn, 7)
            nc.tensor.matmul(PB[:, 1, 0:D], ones[:, :], bn_row[:, 2, :], start=True, stop=True).then_inc(s_bn_pe, 1)

        @block.scalar
        def _(act):
            for t in range(NT):
                for q, nb in ((0, 4), (1, BT - 4)):
                    act.wait_ge(s_rowxw, 2 * t + q + 1)
                    if t >= 2 and q == 0:
                        act.wait_ge(s_rowst[t % 2], 16 * (t // 2))
                    nc.scalar.copy(xwS[:, T8 * (t % 2) + 4 * q:T8 * (t % 2) + 4 * q + nb, :], PB[:, 2 * (t % 2) + q, 0:nb * P].rearrange("p (b n) -> p b n", n=P)).then_inc(s_rowev, 1)
            act.wait_ge(s_tab, 8)
            with nc.allow_non_contiguous_dma(reason="896 counts, once"):
                act.dma_start(start_d.rearrange("c p -> p c"), start_i[:, :]).then_inc(s_start_st, 16)
            act.wait_ge(s_start_st, 16)
            act.dma_start(start_tab[:, :].rearrange("o (c p) -> o c p", p=P), start_d.rearrange("(o c) p -> o c p", o=1)).then_inc(s_in["start"], 16)
            act.wait_ge(s_const, 2)
            act.dma_start(x[:, 0:NB - 1, :], x_d[0:(NB - 1) * P, :].rearrange("(b p) f -> p b f", p=P)).then_inc(s_in["x"], 16)
            act.dma_start(x[0:LAST, NB - 1, :], x_d[(NB - 1) * P:N, :]).then_inc(s_in["x"], 16)
            act.dma_start(vecs[:, :, :], vec_d.broadcast_to([P, 8, D])).then_inc(s_in["vecs"], 16)
            act.wait_ge(s_off, 10)

            def one_hot_window(h, base, n):
                for t in range(T8):
                    last = nc.scalar.activation(dist[:, T8 * h + t, :], win_cols[:, :], ACT.Abs, bias=rel[:, bass.ds(base + t, 1)])
                last.then_inc(s_dist, 1)
                act.wait_ge(s_dist, n + 1)
                nc.scalar.activation(hot_win[:, T8 * h:T8 * h + T8, :], dist[:, T8 * h:T8 * h + T8, :], ACT.Relu, scale=-1.0, bias=eps_ln[:, 0:1]).then_inc(s_hotw, 1)

            def keys_from_groups(h, base):
                _, first_tile = nc.values_load_multi_w_load_instructions(start_tab[0:1, bass.ds(base, GH)], engines=ACT_ONLY, min_val=0, max_val=T - 1,
                                                                         skip_runtime_bounds_check_because="a count of tiles, less one")
                for j in range(GH):
                    nc.scalar.activation(rel_key[:, GH * h + j, :], key[:, bass.ds(first_tile[j], GT)], ACT.Identity,
                                         bias=neg_group_key[:, bass.ds(base + j, 1)]).then_inc(s_rel[h], 1)

            one_hot_window(0, 0, 0)
            keys_from_groups(0, 0)
            with act.Fori(0, NI) as i:
                for h in range(2):
                    act.wait_ge(s_ast[h], i * 16)
                    for j in range(GH):
                        if j == 0:
                            act.wait_ge(s_win[1 - h], i + h)
                            one_hot_window(1 - h, i * (2 * T8) + T8 * (h + 1), 2 * i + (h + 1))
                            keys_from_groups(1 - h, i * (2 * GH) + GH * (h + 1))
                        if j == 0:
                            act.wait_ge(s_win[h], i + 1)
                        act.wait_ge(s_amm[h], i * (GH * GT) + GT * (j + 1))
                        nc.scalar.copy(stage[:, h, :].rearrange("p (b d) -> p b d", d=SN)[:, :, GN * j:GN * j + GN],
                                       PB[:, 4 + j, 0:W].rearrange("p (b d) -> p b d", d=GN)).then_inc(s_aev[j], 1)
                    act.wait_ge(s_aev[GH - 1], 2 * i + h + 1)
                    act.dma_start(at_d[bass.ds(2 * i + h, 1), :, :].rearrange("o p n -> (o p) n"), stage[:, h, :]).then_inc(s_ast[h], 16)

            for h in range(2):
                act.wait_ge(s_add[h], NI)
                act.wait_ge(s_ast[h], 16 * NI)
            act.wait_ge(s_in["vecs"], 16)

            def norm(k):
                if k == 1:
                    act.wait_ge(s_fin["stats"], 3 * NT)
                elif k == 4:
                    act.wait_ge(s_bn, 11 + NT + 1)
                else:
                    for c in range(2):
                        act.wait_ge(S[f"stats{c}"], 3 * of(k, c, 0))
                nc.scalar.activation(rstd[:, :], mean_var[:, :, 1], ACT.Sqrt, bias=eps_ln[:, 1:2]).then_inc(s_norm["sqrt"], 1)

            def rows(k, t, s, p):
                Wk = s_walk[k]
                for n in {1: ("tp", "xs", "yb"), 2: ("xs", "yb"), 3: ("tp", "xs"), 4: ()}[k]:
                    act.wait_ge(Wk[f"{n}{s}"], p)
                if k >= 3:
                    act.wait_ge(Wk[f"st{s}"], 16 * p)
                for b in range(BT):
                    last = nc.scalar.activation(xn[s][:, b, :], BN_SRC[k][:, bass.ds(t * BT + b, 1), :].rearrange("p o f -> p (o f)"), ACT.Identity,
                                                scale=rstd[:, bass.ds(t * BT + b, 1)], bias=shift[:, bass.ds(t * BT + b, 1)])
                last.then_inc(Wk[f"xn{s}"], 1)

            for k in (1, 2, 3):
                Wk = s_walk[k]
                norm(k)
                act.wait_ge(s_norm["ready"], k)

                def high_part(t, s, p):
                    act.wait_ge(Wk[f"xs{s}"], p + 1)
                    nc.scalar.copy(blocks(parts_v[0], t), xs[s]).then_inc(Wk[f"hi{s}"], 1)

                walk_ahead(act, lambda t, s, p: rows(k, t, s, p), high_part)
                act.wait_ge(Wk["lo"], NT)
                if k == 1:
                    act.wait_ge(Wk["lin"], NT)
                for s in range(2):
                    if k < 3:
                        act.wait_ge(Wk[f"yb{s}"], TURNS[s])
                    else:
                        act.wait_ge(Wk[f"st{s}"], 16 * TURNS[s])

                def dense(p, cs, nb):
                    n = nb * P
                    if k == 1:
                        for c in cs:
                            act.wait_ge(S[f"at{c}"], 16 * of(k, c, p + 1))
                            for b in range(SB):
                                act.wait_ge(s_deg[f"sum{c}"], p * SB + max(b - 1, 0))
                                nc.scalar.activation(waste[:, c, b % 2, 0:n].rearrange("p (c d) -> p c d", d=SN), at_v[c][:, 0:n // SN, b, :], ACT.Copy,
                                                     accum_out=sdeg_part[:, bass.ds(2 * p + c, 1), b]).then_inc(s_deg[f"sum{c}"], 1)
                    for c in cs:
                        act.wait_ge(S[f"main{c}"], of(k, c, p + 1))
                        act.wait_ge(S[f"lin{c}"], of(k, c, p))
                        nc.scalar.copy(aggT[c][:, 0:n], PB[:, c, 0:n]).then_inc(S[f"evac{c}"], 1)
                    if k == 3:
                        for c in cs:
                            act.wait_ge(S[f"y{c}"], of(k, c, p + 1))
                            nc.scalar.activation(zpre[c][:, 0:n], zpre[c][:, 0:n], ACT.Tanh).then_inc(s_gated[f"z{c}"], 1)
                        for c in cs:
                            act.wait_ge(s_gated[f"zt{c}"], p + 1)
                            act.wait_ge(s_gated[f"gate{c}"], p)
                            nc.scalar.copy(zT[c][:, 0:n], PB[:, 2 + c, 0:n]).then_inc(s_gated[f"zts{c}"], 1)
                        for c in cs:
                            act.wait_ge(s_gated[f"gate{c}"], p + 1)
                            act.wait_ge(s_gated[f"mix{c}"], 5 * p + 1)
                            nc.scalar.activation(gate[c][:, 0:n], gate[c][:, 0:n], ACT.Sigmoid).then_inc(s_gated[f"g{c}"], 1)

                chunks(act, dense)
                if k == 1:
                    act.wait_ge(s_root, 4)
                    nc.scalar.activation(roots, roots, ACT.Sqrt).then_inc(s_root, 1)
            act.wait_ge(s_bn, 6)
            nc.scalar.activation(sq, y[:, :, :], ACT.Square).then_inc(s_bn_act, 1)
            act.wait_ge(s_bn_pe, 2)
            nc.scalar.activation(bn_row[:, 3, :], PB[:, 1, 0:D], ACT.Sqrt, scale=1.0 / N, bias=eps_ln[:, 1:2]).then_inc(s_bn_act, 1)
            norm(4)
            act.wait_ge(s_norm["ready"], 4)
            walk(act, lambda t, s, p: rows(4, t, s, p))


def layout(a):
    import numpy as np

    x = np.asarray(a["x"])
    xT = np.zeros((D, NP), np.float32)
    xT[:, :N] = x.T
    src = np.zeros(T * P, np.int32)
    src[:E] = a["src"]
    dst = np.full(T * P, NP, np.int32)
    dst[:E] = a["dst"]
    ea = np.zeros(((NH + 1) * T8 * P, ED), np.float32)
    ea[:E] = a["edge_attr_16"]
    w = np.zeros((8, D, D), np.float32)
    w[0] = a["L0_gnn_W"]
    w[1] = np.asarray(a["L1_gnn_W_l"]).T
    w[2] = np.asarray(a["L1_gnn_W_r"]).T
    w[3] = a["L2_gnn_weight"]
    w[4] = a["L3_gnn_gcn_w"]
    w[5] = a["L3_gnn_lin_w"]
    w[6] = a["L3_gnn_gate_w"]
    w[7, :ED] = a["L0_gnn_edge_w"]
    vec = np.stack([np.asarray(a[n]) for n in ("L0_gnn_b", "L1_gnn_b_l", "L2_gnn_bias", "L3_gnn_gcn_b", "L3_gnn_lin_b",
                                               "L3_gnn_gate_b", "L3_gnn_bn_gamma", "L3_gnn_bn_beta")])[None]
    return {
        "in_xT": xT,
        "in_x": np.ascontiguousarray(x),
        "in_ea": np.ascontiguousarray(ea.reshape(NH + 1, T8, P, ED).transpose(0, 1, 3, 2).reshape(NH + 1, T8 * ED, P)),
        "in_idx": np.ascontiguousarray(src.reshape(NH, T8, P).transpose(0, 2, 1)),
        "in_src": np.ascontiguousarray(src.reshape(T, P).T),
        "in_dst": np.ascontiguousarray(dst.reshape(T, P).T),
        "in_next": np.ascontiguousarray(np.append(dst[1:], NP).astype(np.int32).reshape(T, P).T),
        "in_first": np.ascontiguousarray(dst.reshape(T, P)[:, 0][None]),
        "in_half": np.ascontiguousarray(dst.reshape(NH, T8 * P)[:, 0][None]),
        "in_w": w,
        "in_vec": np.ascontiguousarray(vec),
    }


def kernel(**inputs):
    import concourse.bacc as bacc
    from concourse.bass_utils import run_bass_kernel_spmd

    arrays = layout(inputs)
    nc = bacc.Bacc("TRN2", target_bir_lowering=False, num_devices=1)
    ins = [nc.dram_tensor(n, a.shape, mybir.dt.from_np(a.dtype), kind="ExternalInput").ap() for n, a in arrays.items()]
    out = nc.dram_tensor("out", (N, D), F32, kind="ExternalOutput").ap()
    build(nc, *ins, out)
    r = run_bass_kernel_spmd(nc, [arrays], core_ids=[0])
    return r.results[0]["out"]
```
